# Optimizing a Trainium2 kernel written in Bass

```python
import numpy as np
import jax
import jax.numpy as jnp

def _softmax(x, axis=-1):
    return jax.nn.softmax(x, axis=axis)

def _gelu(x):
    return jax.nn.gelu(x, approximate=True)

def _silu(x):
    return jax.nn.silu(x)

def _sigmoid(x):
    return jax.nn.sigmoid(x)

def _layernorm(x, axis=-1, eps=1e-05):
    m = jnp.mean(x, axis=axis, keepdims=True)
    v = jnp.var(x, axis=axis, keepdims=True)
    return (x - m) / jnp.sqrt(v + eps)

def _scatter_add(tgt, idx, src, axis=0):
    return tgt.at[idx].add(src)

def _segment_sum(src, seg, n):
    return jax.ops.segment_sum(src, seg, n)
kernel_name = 'mk_vit_tower_cls_d1_tok_img768_r4_731d1c'

def setup_inputs(seed: int=0):
    np.random.seed(seed)
    _w = jnp.asarray

    def _rec_inputs():
        import jax
        import jax.numpy as jnp
        _rk = jax.random.key(seed)
        x = 7.57192e-06 + 1.00007 * jax.random.normal(jax.random.fold_in(_rk, 1), (32, 64, 64, 3), jnp.float32)
        cls_tok = 0.02 * jax.random.normal(jax.random.fold_in(_rk, 5), (1, 1, 192), jnp.float32)
        return (x, cls_tok)
    x, cls_tok = _rec_inputs()

    def _L0_tok_setup():
        import jax, jax.numpy as jnp
        import numpy as np
        PATCH_SIZES = (8, 16, 32)
        PROJ_DIM = 192
        C = 3

        def _extract_patches(images, p):
            B, H, W, Cc = images.shape
            nh, nw = (H // p, W // p)
            x = images.reshape(B, nh, p, nw, p, Cc)
            x = x.transpose(0, 1, 3, 2, 4, 5)
            return x.reshape(B, nh * nw, p * p * Cc)
        key = jax.random.key(seed)
        ks = jax.random.split(key, 1 + 2 * len(PATCH_SIZES))
        images = jax.random.normal(ks[0], (64, 224, 224, C), dtype=jnp.float32)
        inp = {'images': images}
        for i, p in enumerate(PATCH_SIZES):
            k_in = p * p * C
            scale = 1.0 / np.sqrt(k_in)
            inp[f'W{i}'] = jax.random.uniform(ks[1 + 2 * i], (k_in, PROJ_DIM), dtype=jnp.float32, minval=-scale, maxval=scale)
            inp[f'b{i}'] = jnp.zeros((PROJ_DIM,), dtype=jnp.float32)
        return inp
    _L0_tok_all = _L0_tok_setup()
    _L0_tok_in = {k: v for k, v in _L0_tok_all.items() if k in ('W0', 'b0', 'W1', 'b1', 'W2', 'b2')}
    del _L0_tok_all

    def _L0_attn_setup():
        import jax, jax.numpy as jnp
        import numpy as np
        B, T, D = (2, 512, 192)
        H, K, V = (8, 64, 96)
        F = 32

        def positional_features(positions, feature_size, seq_length):
            nb = feature_size // 2
            pow_rate = np.exp(np.log(seq_length + 1) / nb).astype(np.float32)
            center_widths = pow_rate ** jnp.arange(1, nb + 1, dtype=jnp.float32) - 1.0
            emb = (center_widths[None, :] > jnp.abs(positions)[:, None]).astype(jnp.float32)
            return jnp.concatenate([emb, jnp.sign(positions)[:, None] * emb], axis=-1)

        def relative_shift(x):
            b, h, t1, t2 = x.shape
            x = jnp.pad(x, ((0, 0), (0, 0), (0, 0), (1, 0)))
            x = x.reshape(b, h, t2 + 1, t1)[:, :, 1:, :].reshape(b, h, t1, t2)
            return x[..., :(t2 + 1) // 2]
        key = jax.random.key(seed)
        ks = jax.random.split(key, 9)
        w = lambda k, shape: jax.random.normal(k, shape, jnp.float32) * 0.02
        return {'x': jax.random.normal(ks[0], (B, T, D), jnp.float32), 'Wq': w(ks[1], (D, H * K)), 'Wk': w(ks[2], (D, H * K)), 'Wv': w(ks[3], (D, H * V)), 'Wrk': w(ks[4], (F, H * K)), 'r_w_bias': w(ks[5], (H, K)), 'r_r_bias': w(ks[6], (H, K)), 'Wo': w(ks[7], (H * V, D)), 'bo': jnp.zeros((D,), jnp.float32)}
    _L0_attn_all = _L0_attn_setup()
    _L0_attn_in = {k: v for k, v in _L0_attn_all.items() if k in ('Wq', 'Wk', 'Wv', 'Wrk', 'r_w_bias', 'r_r_bias', 'Wo', 'bo')}
    del _L0_attn_all

    def _L0_ffn_setup():
        import jax, jax.numpy as jnp
        import numpy as np
        B, S, D_IN, D_HID, D_OUT = (32, 128, 192, 768, 192)
        key = jax.random.key(seed)
        k1, k2, k3, k4 = jax.random.split(key, 4)
        init_k = float(np.sqrt(1.0 / D_IN))
        init_k2 = float(np.sqrt(1.0 / D_HID))
        x = jax.random.normal(k1, (B, S, D_IN), dtype=jnp.float32)
        in_weight = jax.random.uniform(k2, (D_HID, D_IN), dtype=jnp.float32, minval=-init_k, maxval=init_k)
        in_bias = jax.random.uniform(k3, (D_HID,), dtype=jnp.float32, minval=-init_k, maxval=init_k)
        out_weight = jax.random.uniform(k4, (D_HID, D_OUT), dtype=jnp.float32, minval=-init_k2, maxval=init_k2)
        return {'x': x, 'in_weight': in_weight, 'in_bias': in_bias, 'out_weight': out_weight}
    _L0_ffn_all = _L0_ffn_setup()
    _L0_ffn_in = {k: v for k, v in _L0_ffn_all.items() if k in ('in_weight', 'in_bias', 'out_weight')}
    del _L0_ffn_all
    return {'x': x, 'cls_tok': cls_tok, 'L0_tok_W0': _L0_tok_in['W0'], 'L0_tok_b0': _L0_tok_in['b0'], 'L0_tok_W1': _L0_tok_in['W1'], 'L0_tok_b1': _L0_tok_in['b1'], 'L0_tok_W2': _L0_tok_in['W2'], 'L0_tok_b2': _L0_tok_in['b2'], 'L0_attn_Wq': _L0_attn_in['Wq'], 'L0_attn_Wk': _L0_attn_in['Wk'], 'L0_attn_Wv': _L0_attn_in['Wv'], 'L0_attn_Wrk': _L0_attn_in['Wrk'], 'L0_attn_r_w_bias': _L0_attn_in['r_w_bias'], 'L0_attn_r_r_bias': _L0_attn_in['r_r_bias'], 'L0_attn_Wo': _L0_attn_in['Wo'], 'L0_attn_bo': _L0_attn_in['bo'], 'L0_ffn_in_weight': _L0_ffn_in['in_weight'], 'L0_ffn_in_bias': _L0_ffn_in['in_bias'], 'L0_ffn_out_weight': _L0_ffn_in['out_weight']}

def reference(x, cls_tok, L0_tok_W0, L0_tok_b0, L0_tok_W1, L0_tok_b1, L0_tok_W2, L0_tok_b2, L0_attn_Wq, L0_attn_Wk, L0_attn_Wv, L0_attn_Wrk, L0_attn_r_w_bias, L0_attn_r_r_bias, L0_attn_Wo, L0_attn_bo, L0_ffn_in_weight, L0_ffn_in_bias, L0_ffn_out_weight):
    import jax
    import jax.numpy as jnp

    def _L0_tok_ref(images, W0, b0, W1, b1, W2, b2):
        import jax, jax.numpy as jnp
        import numpy as np
        PATCH_SIZES = (8, 16, 32)
        PROJ_DIM = 192
        C = 3

        def _extract_patches(images, p):
            B, H, W, Cc = images.shape
            nh, nw = (H // p, W // p)
            x = images.reshape(B, nh, p, nw, p, Cc)
            x = x.transpose(0, 1, 3, 2, 4, 5)
            return x.reshape(B, nh * nw, p * p * Cc)
        Ws = (W0, W1, W2)
        bs = (b0, b1, b2)
        outs = []
        for p, W, b in zip(PATCH_SIZES, Ws, bs):
            patches = _extract_patches(images, p)
            outs.append(jnp.einsum('bnk,kd->bnd', patches, W) + b)
        return jnp.concatenate(outs, axis=1)

    def _L0_attn_ref(x, Wq, Wk, Wv, Wrk, r_w_bias, r_r_bias, Wo, bo):
        import jax, jax.numpy as jnp
        import numpy as np
        B, T, D = (2, 512, 192)
        H, K, V = (8, 64, 96)
        F = 32

        def positional_features(positions, feature_size, seq_length):
            nb = feature_size // 2
            pow_rate = np.exp(np.log(seq_length + 1) / nb).astype(np.float32)
            center_widths = pow_rate ** jnp.arange(1, nb + 1, dtype=jnp.float32) - 1.0
            emb = (center_widths[None, :] > jnp.abs(positions)[:, None]).astype(jnp.float32)
            return jnp.concatenate([emb, jnp.sign(positions)[:, None] * emb], axis=-1)

        def relative_shift(x):
            b, h, t1, t2 = x.shape
            x = jnp.pad(x, ((0, 0), (0, 0), (0, 0), (1, 0)))
            x = x.reshape(b, h, t2 + 1, t1)[:, :, 1:, :].reshape(b, h, t1, t2)
            return x[..., :(t2 + 1) // 2]
        b, t, _ = x.shape
        q = (x @ Wq).reshape(b, t, H, K).transpose(0, 2, 1, 3) * K ** (-0.5)
        k = (x @ Wk).reshape(b, t, H, K).transpose(0, 2, 1, 3)
        v = (x @ Wv).reshape(b, t, H, V).transpose(0, 2, 1, 3)
        content = jnp.einsum('bhtk,bhsk->bhts', q + r_w_bias[None, :, None, :], k)
        positions = jnp.arange(-t + 1, t, dtype=jnp.float32)
        pos_emb = positional_features(positions, F, t)
        r_k = (pos_emb @ Wrk).reshape(2 * t - 1, H, K)
        rel = jnp.einsum('bhtk,rhk->bhtr', q + r_r_bias[None, :, None, :], r_k)
        rel = relative_shift(rel)
        attn = jax.nn.softmax(content + rel, axis=-1)
        out = jnp.einsum('bhts,bhsv->bhtv', attn, v)
        out = out.transpose(0, 2, 1, 3).reshape(b, t, H * V)
        return out @ Wo + bo

    def _L0_ffn_ref(x, in_weight, in_bias, out_weight):
        import jax, jax.numpy as jnp
        import numpy as np
        B, S, D_IN, D_HID, D_OUT = (32, 128, 192, 768, 192)
        lead = x.shape[:-1]
        xt = x.reshape(-1, in_weight.shape[1])
        h = jax.nn.gelu(jnp.einsum('td,hd->th', xt, in_weight) + in_bias, approximate=False)
        out = jnp.einsum('th,ho->to', h, out_weight)
        return out.reshape(*lead, out_weight.shape[1])
    h = _L0_tok_ref(x, L0_tok_W0, L0_tok_b0, L0_tok_W1, L0_tok_b1, L0_tok_W2, L0_tok_b2)
    h = jnp.concatenate([jnp.broadcast_to(cls_tok, (h.shape[0], 1, h.shape[2])), h], axis=1)
    h = h + _L0_attn_ref(_layernorm(h, axis=-1), L0_attn_Wq, L0_attn_Wk, L0_attn_Wv, L0_attn_Wrk, L0_attn_r_w_bias, L0_attn_r_r_bias, L0_attn_Wo, L0_attn_bo)
    h = h + _L0_ffn_ref(_layernorm(h, axis=-1), L0_ffn_in_weight, L0_ffn_in_bias, L0_ffn_out_weight)
    return h

_drawn_inputs = setup_inputs


def setup_inputs(seed=0):
    import zlib

    import numpy as np

    out = dict(_drawn_inputs(seed))
    spreads = {'L0_tok_b0': (0.0, 0.1),
     'L0_tok_b1': (0.0, 0.1),
     'L0_tok_b2': (0.0, 0.1),
     'L0_attn_bo': (0.0, 0.1)}
    factors = {'cls_tok': 6.264,
     'L0_attn_Wq': 8.0,
     'L0_attn_Wk': 8.0,
     'L0_attn_Wrk': 8.0,
     'L0_attn_r_w_bias': 8.0,
     'L0_attn_r_r_bias': 8.0}
    for name, (base, spread) in spreads.items():
        noise = np.random.default_rng([zlib.crc32(name.encode()), seed]).standard_normal(out[name].shape)
        drawn = base * np.exp(spread * noise) if base else spread * noise
        out[name] = jnp.asarray(drawn.astype(out[name].dtype))
    for name, factor in factors.items():
        out[name] = (out[name] * factor).astype(out[name].dtype)
    return out
```

```python
from contextlib import ExitStack

import numpy as np

import concourse.bass as bass
from concourse import mybir

F32 = mybir.dt.float32
ALU = mybir.AluOpType
ACT = mybir.ActivationFunctionType
AX = mybir.AxisListType

B, IMG, CH = 32, 64, 3
D = 192
H, KD, VD, RF = 8, 64, 96, 32
HID = 768
PATCHES = (8, 16, 32)
GRIDS = tuple(IMG // p for p in PATCHES)
FIRST_TOKEN = (1, 1 + GRIDS[0] ** 2, 1 + GRIDS[0] ** 2 + GRIDS[1] ** 2)
T = FIRST_TOKEN[2] + GRIDS[2] ** 2
EPS = 1e-5
QSCALE = KD ** -0.5

KC = 2
DK = D // KC
G = 4
NQ = B // G
NT = G * T
TILE = 114
TILES = [(j * TILE, min(TILE, NT - j * TILE)) for j in range(-(-NT // TILE))]
HH = H // 2
HALVES = 2 * G
HT = HH * T
J = 4
RG = -(-T // J)
RWIN = 2 * T - 1
RBATCH = 4
RBATCHES = -(-RG // RBATCH)
HB = H * G
QM = H * KD // 128
MH = HID // 128
PIX = PATCHES[0] ** 2 * CH
SUB = (PATCHES[2] // PATCHES[0]) ** 2
NB = B * GRIDS[2] ** 2

PRE_XT, PRE_QK, PRE_V, PRE_U, PRE_REL = 0, 2, 2 + 2 * QM, 2 + 2 * QM + 2 * G, 4 + 2 * QM + 2 * G
PRE_USES = PRE_REL + RBATCHES
POST_WO, POST_XT, POST_UP, POST_DOWN = 0, 3, 5, 5 + MH
POST_USES = POST_DOWN + 3
assert PRE_USES % 2 == 0 and POST_USES % 2 == 0 and NB == 128


def positional_windows():
    nb = RF // 2
    rate = np.exp(np.log(T + 1) / nb).astype(np.float32)
    widths = rate ** np.arange(1, nb + 1, dtype=np.float32) - np.float32(1)
    pos = np.arange(RWIN)[None, :] - np.arange(J)[:, None] - (T - 1)
    inside = (widths[None, :, None] > np.abs(pos)[:, None, :]).astype(np.float32)
    signed = np.sign(pos)[:, None, :] * inside
    return np.concatenate([inside, signed], axis=1).reshape(J * RF, RWIN).astype(np.float32)


def build(nc, ins, out):
    with ExitStack() as ctx:
        def sb(name, shape):
            return ctx.enter_context(nc.sbuf_tensor(name, shape, F32))

        def psum(name):
            return ctx.enter_context(nc.psum_tensor(name, [128, 512], F32))

        def sem(name):
            return ctx.enter_context(nc.semaphore(name))

        w_tok0 = sb("w_tok0", [DK, KC, D])
        w_tok1 = sb("w_tok1", [DK, KC, 4, D])
        b_tok = sb("b_tok", [128, 3, D])
        w_q = sb("w_q", [DK, KC, H * KD])
        w_k = sb("w_k", [DK, KC, H * KD])
        w_v = sb("w_v", [DK, KC, H * VD])
        w_qt = sb("w_qt", [KD, H, D])
        w_rkt = sb("w_rkt", [KD, H, RF])
        rw_bias = sb("rw_bias", [128, QM])
        rr_bias = sb("rr_bias", [KD, H])
        w_o = sb("w_o", [VD, H, D])
        b_o = sb("b_o", [128, D])
        w_in = sb("w_in", [DK, KC, HID])
        b_in = sb("b_in", [128, MH])
        w_out = sb("w_out", [128, MH, D])
        ident = sb("ident", [128, 128])
        windows = sb("windows", [J * RF, RWIN])
        w_u = sb("w_u", [DK, KC, H, RF])
        u_bias = sb("u_bias", [J * RF, H])

        neg_half = sb("neg_half", [128, 3])
        eps = sb("eps", [128, 3])
        spare = sb("spare", [1, 2])

        arena_v = sb("arena_v", [128, 2 * G * H * VD])
        v_sb = arena_v[:, :].rearrange("p (r i h v) -> p r i h v", r=2, i=G, h=H)
        w_tok2 = arena_v[0:DK, 0:KC * SUB * D].rearrange("p (k s d) -> p k s d", k=KC, s=SUB)
        arena_r = sb("arena_r", [128, 2 * HB * T])
        rel_sb = arena_r[:, :].rearrange("p (r n t) -> p r n t", r=2, n=HB)
        pix = arena_r[0:DK, 0:KC * SUB * NB].rearrange("p (k s n) -> p k s n", k=KC, s=SUB)
        TOK_RING = 4
        tok_sb = sb("tok_sb", [128, TOK_RING, D])

        h_in = sb("h_in", [128, 2, 3, D])
        h_bo = sb("h_bo", [128, 2, 3, D])
        ln1_stats = sb("ln1_stats", [128, 3, 6])
        ln1_mv = sb("ln1_mv", [128, 3, 2])
        ln1_rstd = sb("ln1_rstd", [128, 3])
        xn = sb("xn", [128, 3, D])
        xnt = sb("xnt", [DK, KC, NT])
        q_sb = sb("q_sb", [128, 2, QM, NT])
        k_sb = sb("k_sb", [128, 2, QM, NT])
        u_diag = sb("u_diag", [J * RF, J, H, G, RG])
        st_sb = sb("st_sb", [T, 2, HH, T])
        smax = sb("smax", [T, 2, HH])
        shifted = sb("shifted", [T, 2, HH, T])
        prob = sb("prob", [T, 2, HH, T])
        psums = sb("psums", [T, 2, HH])
        precip = sb("precip", [T, 2, HH])
        probn = sb("probn", [T, 2, HH, T])
        pt_sb = sb("pt_sb", [T, 2, HH, T])
        ot_sb = sb("ot_sb", [VD, H, NT])
        h1 = sb("h1", [128, 3, D])
        ln2_stats = sb("ln2_stats", [128, 3, 6])
        ln2_mv = sb("ln2_mv", [128, 3, 2])
        ln2_rstd = sb("ln2_rstd", [128, 3])
        x2 = sb("x2", [128, 3, D])
        x2t = sb("x2t", [DK, KC, NT])
        hid = sb("hid", [128, MH, NT])
        y_sb = sb("y_sb", [128, 3, D])

        st_ps, s_ps, pt_ps, ot_ps = (psum(n) for n in ("st_ps", "s_ps", "pt_ps", "ot_ps"))
        pre_ps = [psum("pre_ps0"), psum("pre_ps1")]
        post_ps = [psum("post_ps0"), psum("post_ps1")]
        tok_ps = [pre_ps[0], pre_ps[1], post_ps[0], post_ps[1]]

        h_dram = nc.dram_tensor("h_scratch", (B, T, D), F32, kind="Internal").ap()
        h_rows = h_dram.rearrange("b t d -> (b t) d")
        out_rows = out.rearrange("b t d -> (b t) d")

        ld = {n: sem("ld_" + n) for n in (
            "w0", "pix", "w1", "w2", "btok", "qk", "v", "u", "rwb", "o", "in", "out", "const")}
        tok_mm = sem("tok_mm")
        tok_add = sem("tok_add")
        tok_wr = [sem(f"tok_wr{i}") for i in range(TOK_RING)]
        cls_wr = sem("cls_wr")
        cleared = sem("cleared")
        u_mm = sem("u_mm")
        u_ready = sem("u_ready")
        h_ld = [sem("h_ld0"), sem("h_ld1")]
        hbo_done = sem("hbo_done")
        ln1_step = sem("ln1_step")
        ln2_step = sem("ln2_step")
        ln1_rstd_step = sem("ln1_rstd_step")
        ln2_rstd_step = sem("ln2_rstd_step")
        pre_full = [sem("pre_full0"), sem("pre_full1")]
        pre_evac = [sem("pre_evac0"), sem("pre_evac1")]
        post_full = [sem("post_full0"), sem("post_full1")]
        post_evac = [sem("post_evac0"), sem("post_evac1")]
        st_full, st_evac = sem("st_full"), sem("st_evac")
        s_full = sem("s_full")
        max_done = sem("max_done")
        s_evac = sem("s_evac")
        exp_done = sem("exp_done")
        sum_done = sem("sum_done")
        recip_done = sem("recip_done")
        probn_done = sem("probn_done")
        pt_full, pt_evac = sem("pt_full"), sem("pt_evac")
        ot_full, ot_evac = sem("ot_full"), sem("ot_evac")
        y_out = sem("y_out")

        block = ctx.enter_context(nc.Block())

        def wait(eng, s, value):
            if isinstance(value, int) and value <= 0:
                return
            eng.wait_ge(s, value)

        def pre_count(q, n):
            return q * (PRE_USES // 2) + (n // 2 + 1)

        def post_count(q, n):
            return q * (POST_USES // 2) + (n // 2 + 1)

        def lagged(q, par, slot, lag):
            if slot >= lag:
                return None if isinstance(q, int) and q == NQ else (q, par, slot - lag, q * HALVES + (slot - lag))
            if isinstance(q, int) and q == 0:
                return None
            k = slot - lag + HALVES
            return (q - 1, 1 - par, k, q * HALVES + (slot - lag))

        def a_parity(where):
            return where[2] % 2

        def rel_copies(par, r):
            bank = pre_ps[(PRE_REL + r) % 2]
            first = r * RBATCH
            whole = min(RBATCH, T // J - first)
            pairs = [(rel_sb[0:T, par, :, J * first:J * (first + whole)].rearrange("p n (g j) -> p n g j", j=J),
                      bank[0:T, 0:whole * J * HB].rearrange("p (g j n) -> p n g j", g=whole, j=J))]
            if first + whole < min(first + RBATCH, RG):
                js = T - J * (first + whole)
                pairs.append((rel_sb[0:T, par, :, J * (first + whole):T],
                              bank[0:T, whole * J * HB:(whole * J + js) * HB].rearrange("p (j n) -> p n j", j=js)))
            return pairs

        def passes(eng, iteration, tail):
            iteration(0, 0, pre=True, post=False)
            with eng.Fori(1, NQ - 1, 2) as q:
                iteration(q, 1, pre=True, post=True)
                iteration(q + 1, 0, pre=True, post=True)
            iteration(NQ - 1, 1, pre=False, post=True)
            tail(NQ, 0)

        @block.sync
        def _(sp):
            sp.dma_start(w_tok0[:, :, :], ins["w0"]).then_inc(ld["w0"], 16)
            sp.dma_start(pix[:, 0], ins["pix"][:, 0]).then_inc(ld["pix"], 16)
            sp.dma_start(pix[:, 1], ins["pix"][:, 1]).then_inc(ld["pix"], 16)
            sp.dma_start(b_tok[:, :, :], ins["b_tok"]).then_inc(ld["btok"], 16)
            sp.dma_start(w_tok1[:, :, :, :], ins["w1"]).then_inc(ld["w1"], 16)
            sp.dma_start(w_tok2, ins["w2"]).then_inc(ld["w2"], 16)
            sp.dma_start(w_qt[:, :, :], ins["w_qt"]).then_inc(ld["u"], 16)
            sp.dma_start(w_rkt[:, :, :], ins["w_rkt"]).then_inc(ld["u"], 16)
            sp.dma_start(rr_bias[:, :], ins["rr_bias"]).then_inc(ld["u"], 16)
            sp.dma_start(ident[:, :], ins["ident"]).then_inc(ld["const"], 16)
            sp.dma_start(windows[:, :], ins["windows"]).then_inc(ld["const"], 16)
            sp.dma_start(b_o[:, :], ins["b_o"]).then_inc(ld["const"], 16)
            sp.dma_start(w_q[:, :, :], ins["w_q"]).then_inc(ld["qk"], 16)
            sp.dma_start(w_k[:, :, :], ins["w_k"]).then_inc(ld["qk"], 16)
            sp.dma_start(rw_bias[:, :], ins["rw_bias"]).then_inc(ld["rwb"], 16)
            sp.dma_start(w_v[:, :, :], ins["w_v"]).then_inc(ld["v"], 16)
            sp.dma_start(w_o[:, :, :], ins["w_o"]).then_inc(ld["o"], 16)
            sp.dma_start(w_in[:, :, :], ins["w_in"]).then_inc(ld["in"], 16)
            sp.dma_start(b_in[:, :], ins["b_in"]).then_inc(ld["in"], 16)
            sp.dma_start(w_out[:, :, :], ins["w_out"]).then_inc(ld["out"], 16)

            def load_quad(q, par):
                wait(sp, ln1_step, (q - 1) * 9)
                wait(sp, hbo_done, q - 1)
                for j, (t0, rows) in enumerate(TILES):
                    sp.dma_start(h_in[0:rows, par, j, :],
                                 h_rows[bass.ds(q * NT + t0, rows), :]).then_inc(h_ld[par], 16)

            def store_quad(q):
                for j, (t0, rows) in enumerate(TILES):
                    sp.wait_ge(post_evac[(POST_DOWN + j) % 2], post_count(q, POST_DOWN + j))
                    sp.dma_start(out_rows[bass.ds(q * NT + t0, rows), :],
                                 y_sb[0:rows, j, :]).then_inc(y_out, 16)

            for i in range(TOK_RING):
                tiles = len(range(i, SUB + 4 + 1, TOK_RING))
                sp.wait_ge(tok_wr[i], 16 * tiles * 2)
            sp.wait_ge(cls_wr, 16)
            sp.wait_ge(cleared, 1)
            load_quad(0, 0)
            load_quad(1, 1)
            load_quad(2, 0)
            with sp.Fori(1, NQ - 3, 1 + 1) as q:
                store_quad(q - 1)
                load_quad(q + 2, 1)
                store_quad(q)
                load_quad(q + 3, 0)
            for q in range(NQ - 3, NQ + 1):
                store_quad(q - 1)
                if q + 2 < NQ:
                    load_quad(q + 2, (q + 2) % 2)
            sp.wait_ge(y_out, NQ * 3 * 16)

        @block.gpsimd
        def _(pool):
            pool.dma_start(h_dram[:, 0, :], ins["cls"]).then_inc(cls_wr, 16)
            nc.gpsimd.memset(neg_half[:, :], -0.5)
            nc.gpsimd.memset(eps[:, :], EPS)
            for buf in (h_in, h_bo, ln1_mv, ln2_mv):
                nc.gpsimd.memset(buf[tuple(slice(None) for _ in buf.shape)], 0.0)
            nc.gpsimd.memset(h1[:, :, :], 0.0).then_inc(cleared, 1)
            nc.gpsimd.memset(u_diag[:, :, :, :, :], 0.0).then_inc(cleared, 1)

            for i in range(SUB + 5):
                pool.wait_ge(tok_add, i + 1)
                scale, first = (0, 0) if i < SUB else (1, SUB) if i < SUB + 4 else (2, SUB + 4)
                side = GRIDS[scale] // GRIDS[2]
                ys, xs = divmod(i - first, side)
                rows = h_dram[:, FIRST_TOKEN[scale]:FIRST_TOKEN[scale] + GRIDS[scale] ** 2, :]
                rows = rows.rearrange("b (Y y X x) d -> y x Y X b d", Y=2, X=2, y=side)[ys, xs]
                for Y in range(2):
                    pool.dma_start(rows[Y],
                                   tok_sb[64 * Y:64 * Y + 64, i % TOK_RING, :]).then_inc(tok_wr[i % TOK_RING], 16)

            def bias_residual(q, par):
                pool.wait_ge(h_ld[par], (q - par) * 24 + 48)
                wait(pool, post_evac[0], post_count(q - 2, POST_WO + 2))
                wait(pool, post_evac[1], post_count(q - 2, POST_WO + 1))
                nc.gpsimd.tensor_tensor(h_bo[:, par], h_in[:, par],
                                        b_o[:, :].unsqueeze(1).to_broadcast([128, 3, D]),
                                        ALU.add).then_inc(hbo_done, 1)

            def rstd(q, step, rstd_step, mv, out):
                pool.wait_ge(step, q * 9 + 6)
                nc.gpsimd.tensor_tensor(out[:, :], mv[:, :, 1], eps[:, :], ALU.add).then_inc(rstd_step, 1)
                pool.wait_ge(rstd_step, 2 * q + 1)
                nc.gpsimd.tensor_tensor(out[:, :], out[:, :], neg_half[:, :], ALU.pow).then_inc(rstd_step, 1)

            def normalize(where):
                if where is None:
                    return
                _, _, _, a = where
                buf = a_parity(where)
                pool.wait_ge(recip_done, a + 1)
                wait(pool, pt_full, a - 1)
                nc.gpsimd.tensor_tensor(probn[:, buf], prob[:, buf],
                                        precip[:, buf].unsqueeze(2).to_broadcast([T, HH, T]),
                                        ALU.mult).then_inc(probn_done, 1)

            def iteration(q, par, pre, post):
                for slot in range(HALVES):
                    if slot == 4 and pre:
                        bias_residual(q + 1, 1 - par)
                    if slot == 0 and pre:
                        rstd(q + 1, ln1_step, ln1_rstd_step, ln1_mv, ln1_rstd)
                    if slot == 3 and post:
                        rstd(q - 1, ln2_step, ln2_rstd_step, ln2_mv, ln2_rstd)
                    normalize(lagged(q, par, slot, 1))

            pool.wait_ge(ld["const"], 48)
            bias_residual(0, 0)
            rstd(0, ln1_step, ln1_rstd_step, ln1_mv, ln1_rstd)

            def tail(q, par):
                normalize(lagged(q, par, 0, 1))
                rstd(q - 1, ln2_step, ln2_rstd_step, ln2_mv, ln2_rstd)

            passes(pool, iteration, tail)

        @block.tensor
        def _(pe):
            def tok_tile(i, products):
                bank = tok_ps[i % 4]
                wait(pe, tok_add, i - 3)
                for n, (lhs, rhs) in enumerate(products):
                    last = nc.tensor.matmul(bank[:, 0:D], lhs, rhs, start=(n == 0),
                                            stop=(n == len(products) - 1))
                last.then_inc(tok_mm, 1)

            pe.wait_ge(ld["w0"], 16)
            pe.wait_ge(ld["pix"], 32)
            for s in range(SUB):
                tok_tile(s, [(pix[:, k, s, :], w_tok0[:, k, :]) for k in range(KC)])
            pe.wait_ge(ld["w1"], 16)
            for t in range(4):
                yb, xb = divmod(t, 2)
                tok_tile(SUB + t, [(pix[:, k, (2 * yb + ya) * 4 + 2 * xb + xa, :], w_tok1[:, k, 2 * ya + xa, :])
                                   for ya in range(2) for xa in range(2) for k in range(KC)])
            pe.wait_ge(ld["w2"], 16)
            tok_tile(SUB + 4, [(pix[:, k, s, :], w_tok2[:, k, s, :]) for s in range(SUB) for k in range(KC)])

            pe.wait_ge(ld["u"], 48)
            for h in range(H):
                for k in range(KC):
                    last = nc.tensor.matmul(st_ps[0:DK, (k * H + h) * RF:(k * H + h + 1) * RF],
                                            w_qt[:, h, k * DK:(k + 1) * DK], w_rkt[:, h, :], start=True, stop=True)
            for j in range(J):
                for h in range(H):
                    last = nc.tensor.matmul(s_ps[j * RF:(j + 1) * RF, h:h + 1], w_rkt[:, h, :],
                                            rr_bias[:, h:h + 1], start=True, stop=True)
            last.then_inc(u_mm, 1)

            def pre_use(q, n):
                wait(pe, pre_evac[n % 2], q * (PRE_USES // 2) + n // 2)
                return pre_ps[n % 2]

            def pre_transpose(q):
                pe.wait_ge(ln1_step, (q + 1) * 9)
                for k in range(KC):
                    bank = pre_use(q, PRE_XT + k)
                    for j, (t0, rows) in enumerate(TILES):
                        last = nc.tensor.transpose(bank[0:DK, t0:t0 + rows], xn[0:rows, j, k * DK:(k + 1) * DK],
                                                   ident[0:rows, 0:rows])
                    last.then_inc(pre_full[(PRE_XT + k) % 2], 1)

            def pre_qk(q, tiles):
                for m in tiles:
                    n = PRE_QK + m
                    w = w_q if m < QM else w_k
                    c = (m % QM) * 128
                    bank = pre_use(q, n)
                    if m == 0:
                        for k in range(KC):
                            pe.wait_ge(pre_evac[(PRE_XT + k) % 2], pre_count(q, PRE_XT + k))
                    for k in range(KC):
                        last = nc.tensor.matmul(bank[:, 0:NT], w[:, k, c:c + 128], xnt[:, k, :],
                                                start=(k == 0), stop=(k == KC - 1))
                    last.then_inc(pre_full[n % 2], 1)

            def pre_v(q, img):
                for half in range(2):
                    n = PRE_V + 2 * img + half
                    bank = pre_use(q, n)
                    c = half * HH * VD
                    for k in range(KC):
                        last = nc.tensor.matmul(bank[0:T, 0:HH * VD], xnt[:, k, img * T:(img + 1) * T],
                                                w_v[:, k, c:c + HH * VD], start=(k == 0), stop=(k == KC - 1))
                    last.then_inc(pre_full[n % 2], 1)

            def pre_u(q):
                for half in range(2):
                    n = PRE_U + half
                    bank = pre_use(q, n)
                    for h in range(HH):
                        for j in range(J):
                            count = len(range(j, T, J))
                            o = bank[j * RF:(j + 1) * RF, h * G * RG:(h + 1) * G * RG]
                            o = o.rearrange("p (i g) -> p i g", i=G)[:, :, 0:count]
                            for k in range(KC):
                                x = xnt[:, k, :].rearrange("p (i t) -> p i t", i=G)[:, :, j::J]
                                last = nc.tensor.matmul(o, w_u[:, k, half * HH + h, :], x, start=(k == 0),
                                                        stop=(k == KC - 1))
                    last.then_inc(pre_full[n % 2], 1)

            def pre_rel(q):
                for half in range(2):
                    pe.wait_ge(pre_evac[(PRE_U + half) % 2], pre_count(q, PRE_U + half))
                for r in range(RBATCHES):
                    n = PRE_REL + r
                    bank = pre_use(q, n)
                    for g in range(r * RBATCH, min((r + 1) * RBATCH, RG)):
                        js = min(J, T - g * J)
                        c = (g - r * RBATCH) * J * HB
                        last = nc.tensor.matmul(bank[0:T, c:c + js * HB], windows[:, T - 1 - J * g:2 * T - 1 - J * g],
                                                u_diag[:, 0:js, :, :, g].rearrange("p j h i -> p j (h i)"), start=True, stop=True)
                    last.then_inc(pre_full[n % 2], 1)

            def content(where):
                if where is None:
                    return
                q, par, k, a = where
                img, half = divmod(k, 2)
                if k == 0:
                    for m in (2 * QM - 2, 2 * QM - 1):
                        pe.wait_ge(pre_evac[(PRE_QK + m) % 2], pre_count(q, PRE_QK + m))
                wait(pe, st_evac, a)
                for hh in range(HH):
                    p = KD * half
                    tok = slice(img * T, (img + 1) * T)
                    last = nc.tensor.matmul(st_ps[0:T, hh * T:(hh + 1) * T], k_sb[p:p + KD, par, hh, tok],
                                            q_sb[p:p + KD, par, hh, tok], start=True, stop=True)
                last.then_inc(st_full, 1)

            def scores_transpose(where):
                if where is None:
                    return
                a, buf = where[3], a_parity(where)
                pe.wait_ge(st_evac, a + 1)
                wait(pe, s_evac, a)
                for hh in range(HH):
                    last = nc.tensor.transpose(s_ps[0:T, hh * T:(hh + 1) * T], st_sb[:, buf, hh, :], ident[0:T, 0:T])
                last.then_inc(s_full, 1)

            def probs_transpose(where):
                if where is None:
                    return
                a, buf = where[3], a_parity(where)
                pe.wait_ge(probn_done, a + 1)
                wait(pe, pt_evac, a)
                for hh in range(HH):
                    last = nc.tensor.transpose(pt_ps[0:T, hh * T:(hh + 1) * T], probn[:, buf, hh, :], ident[0:T, 0:T])
                last.then_inc(pt_full, 1)

            def weighted_values(where):
                if where is None:
                    return
                q, par, k, a = where
                img, half = divmod(k, 2)
                if k == 0:
                    for n in (PRE_V + 2 * G - 2, PRE_V + 2 * G - 1):
                        pe.wait_ge(pre_evac[n % 2], pre_count(q, n))
                pe.wait_ge(pt_evac, a + 1)
                wait(pe, ot_evac, a)
                for hh in range(HH):
                    last = nc.tensor.matmul(ot_ps[0:VD, hh * T:(hh + 1) * T], v_sb[0:T, par, img, 2 * hh + half, :],
                                            pt_sb[:, a_parity(where), hh, :], start=True, stop=True)
                last.then_inc(ot_full, 1)

            def post_use(q, n):
                wait(pe, post_evac[n % 2], q * (POST_USES // 2) + n // 2)
                return post_ps[n % 2]

            def post_project(q):
                pe.wait_ge(ot_evac, (q + 1) * HALVES)
                for j, (t0, rows) in enumerate(TILES):
                    n = POST_WO + j
                    bank = post_use(q, n)
                    for h in range(H):
                        last = nc.tensor.matmul(bank[0:rows, 0:D], ot_sb[:, h, t0:t0 + rows], w_o[:, h, :],
                                                start=(h == 0), stop=(h == H - 1))
                    last.then_inc(post_full[n % 2], 1)

            def post_transpose(q):
                pe.wait_ge(ln2_step, (q + 1) * 9)
                for k in range(KC):
                    n = POST_XT + k
                    bank = post_use(q, n)
                    for j, (t0, rows) in enumerate(TILES):
                        last = nc.tensor.transpose(bank[0:DK, t0:t0 + rows], x2[0:rows, j, k * DK:(k + 1) * DK],
                                                   ident[0:rows, 0:rows])
                    last.then_inc(post_full[n % 2], 1)

            def post_up(q):
                for m in range(MH):
                    n = POST_UP + m
                    bank = post_use(q, n)
                    if m == 0:
                        for k in range(KC):
                            pe.wait_ge(post_evac[(POST_XT + k) % 2], post_count(q, POST_XT + k))
                    for k in range(KC):
                        last = nc.tensor.matmul(bank[:, 0:NT], w_in[:, k, m * 128:(m + 1) * 128], x2t[:, k, :],
                                                start=(k == 0), stop=(k == KC - 1))
                    last.then_inc(post_full[n % 2], 1)

            def post_down(q):
                for m in (MH - 2, MH - 1):
                    pe.wait_ge(post_evac[(POST_UP + m) % 2], post_count(q, POST_UP + m))
                for j, (t0, rows) in enumerate(TILES):
                    n = POST_DOWN + j
                    bank = post_use(q, n)
                    for m in range(MH):
                        last = nc.tensor.matmul(bank[0:rows, 0:D], hid[:, m, t0:t0 + rows], w_out[:, m, :],
                                                start=(m == 0), stop=(m == MH - 1))
                    last.then_inc(post_full[n % 2], 1)

            def iteration(q, par, pre, post):
                for slot in range(HALVES):
                    if slot == 3 and post:
                        post_project(q - 1)
                    content(lagged(q, par, slot, 0))
                    scores_transpose(lagged(q, par, slot, 1))
                    probs_transpose(lagged(q, par, slot, 2))
                    weighted_values(lagged(q, par, slot, 3))
                    if pre and slot == 1:
                        pre_transpose(q + 1)
                        pre_qk(q + 1, range(0, QM))
                    if pre and slot == 2:
                        pre_qk(q + 1, range(QM, 2 * QM))
                        pre_v(q + 1, 0)
                    if pre and slot == 3:
                        pre_v(q + 1, 1)
                    if pre and slot == 4:
                        pre_v(q + 1, 2)
                        pre_v(q + 1, 3)
                    if post and slot == 5:
                        post_transpose(q - 1)
                        post_up(q - 1)
                    if pre and slot == 6:
                        pre_u(q + 1)
                        pre_rel(q + 1)
                    if post and slot == 7:
                        post_down(q - 1)

            def tail(q, par):
                for slot in range(3):
                    scores_transpose(lagged(q, par, slot, 1) if slot < 1 else None)
                    probs_transpose(lagged(q, par, slot, 2) if slot < 2 else None)
                    weighted_values(lagged(q, par, slot, 3))
                post_project(q - 1)
                post_transpose(q - 1)
                post_up(q - 1)
                post_down(q - 1)

            pe.wait_ge(ld["const"], 48)
            pre_transpose(0)
            pe.wait_ge(ld["qk"], 32)
            pre_qk(0, range(2 * QM))
            pe.wait_ge(ld["v"], 16)
            for img in range(G):
                pre_v(0, img)
            pe.wait_ge(u_ready, 2)
            pre_u(0)
            pre_rel(0)
            for name, count in (("o", 16), ("in", 32), ("out", 16)):
                pe.wait_ge(ld[name], count)
            passes(pe, iteration, tail)

        @block.scalar
        def _(act):
            def pre_x(q):
                for k in range(KC):
                    n = PRE_XT + k
                    act.wait_ge(pre_full[n % 2], pre_count(q, n))
                    nc.scalar.copy(xnt[:, k, :], pre_ps[n % 2][0:DK, 0:NT]).then_inc(pre_evac[n % 2], 1)

            def pre_q(q, par):
                for m in range(QM):
                    n = PRE_QK + m
                    act.wait_ge(pre_full[n % 2], pre_count(q, n))
                    nc.scalar.activation(q_sb[:, par, m, :], pre_ps[n % 2][:, 0:NT], ACT.Identity,
                                         bias=rw_bias[:, m:m + 1], scale=QSCALE).then_inc(pre_evac[n % 2], 1)

            def pre_v(q, par, img):
                n = PRE_V + 2 * img
                act.wait_ge(pre_full[n % 2], pre_count(q, n))
                nc.scalar.copy(v_sb[0:T, par, img, 0:HH, :],
                               pre_ps[n % 2][0:T, 0:HH * VD]).then_inc(pre_evac[n % 2], 1)

            def pre_rel(q, par):
                for r in range(0, RBATCHES, 2):
                    act.wait_ge(pre_full[(PRE_REL + r) % 2], pre_count(q, PRE_REL + r))
                    for o, i in rel_copies(par, r):
                        last = nc.scalar.copy(o, i)
                    last.then_inc(pre_evac[(PRE_REL + r) % 2], 1)

            def exponentials(where):
                if where is None:
                    return
                a, buf = where[3], a_parity(where)
                act.wait_ge(s_evac, a + 1)
                wait(act, probn_done, a - 1)
                nc.scalar.activation(prob[:, buf], shifted[:, buf], ACT.Exp).then_inc(exp_done, 1)

            def probs_copy(where):
                if where is None:
                    return
                a, buf = where[3], a_parity(where)
                act.wait_ge(pt_full, a + 1)
                wait(act, ot_full, a - 1)
                nc.scalar.copy(pt_sb[:, buf], pt_ps[0:T, 0:HT]).then_inc(pt_evac, 1)

            def outputs_copy(where):
                if where is None:
                    return
                _, _, k, a = where
                img, half = divmod(k, 2)
                act.wait_ge(ot_full, a + 1)
                nc.scalar.copy(ot_sb[:, half::2, img * T:(img + 1) * T],
                               ot_ps[0:VD, 0:HT].rearrange("p (h t) -> p h t", h=HH)).then_inc(ot_evac, 1)

            def post_x(q):
                for k in range(KC):
                    n = POST_XT + k
                    act.wait_ge(post_full[n % 2], post_count(q, n))
                    nc.scalar.copy(x2t[:, k, :], post_ps[n % 2][0:DK, 0:NT]).then_inc(post_evac[n % 2], 1)

            def post_gelu(q):
                for m in range(MH):
                    n = POST_UP + m
                    act.wait_ge(post_full[n % 2], post_count(q, n))
                    nc.scalar.activation(hid[:, m, :], post_ps[n % 2][:, 0:NT], ACT.Gelu,
                                         bias=b_in[:, m:m + 1]).then_inc(post_evac[n % 2], 1)

            def iteration(q, par, pre, post):
                for slot in range(HALVES):
                    exponentials(lagged(q, par, slot, 1))
                    probs_copy(lagged(q, par, slot, 2))
                    outputs_copy(lagged(q, par, slot, 3))
                    if pre and slot == 1:
                        pre_x(q + 1)
                        pre_q(q + 1, 1 - par)
                    if pre and slot == 2:
                        pre_v(q + 1, 1 - par, 0)
                    if pre and slot == 3:
                        pre_v(q + 1, 1 - par, 1)
                    if pre and slot == 4:
                        pre_v(q + 1, 1 - par, 2)
                        pre_v(q + 1, 1 - par, 3)
                    if post and slot == 5:
                        post_x(q - 1)
                        post_gelu(q - 1)
                    if pre and slot == 6:
                        pre_rel(q + 1, 1 - par)

            def tail(q, par):
                for slot in range(3):
                    exponentials(lagged(q, par, slot, 1) if slot < 1 else None)
                    probs_copy(lagged(q, par, slot, 2) if slot < 2 else None)
                    outputs_copy(lagged(q, par, slot, 3))
                post_x(q - 1)
                post_gelu(q - 1)

            pre_x(0)
            act.wait_ge(ld["rwb"], 16)
            pre_q(0, 0)
            for img in range(G):
                pre_v(0, 0, img)
            pre_rel(0, 0)
            act.wait_ge(ld["in"], 32)
            passes(act, iteration, tail)

        @block.vector
        def _(dve):
            dve.wait_ge(ld["btok"], 16)
            for i in range(SUB + 5):
                scale = 0 if i < SUB else 1 if i < SUB + 4 else 2
                dve.wait_ge(tok_mm, i + 1)
                wait(dve, tok_wr[i % TOK_RING], 32 * (i // TOK_RING))
                nc.vector.tensor_tensor(tok_sb[:, i % TOK_RING, :], tok_ps[i % 4][:, 0:D], b_tok[:, scale, :],
                                        ALU.add).then_inc(tok_add, 1)
            dve.wait_ge(u_mm, 1)
            nc.vector.tensor_scalar(w_u[:, :, :, :].rearrange("p k h f -> p (k h f)"), st_ps[0:DK, 0:KC * H * RF],
                                    QSCALE, None, ALU.mult).then_inc(u_ready, 1)
            nc.vector.tensor_copy(u_bias[:, :], s_ps[:, 0:H]).then_inc(u_ready, 1)

            def layer_norm(q, step, rstd_step, src, stats, mv, rstd, dst):
                base = q * 9
                for j, (_, rows) in enumerate(TILES):
                    nc.vector.bn_stats(stats[0:rows, j, :], src[0:rows, j, :]).then_inc(step, 1)
                dve.wait_ge(step, base + 3)
                nc.vector.memset(spare[:, :], 0.0)
                for j, (_, rows) in enumerate(TILES):
                    nc.vector.bn_aggr(mv[0:rows, j, :], stats[0:rows, j, :]).then_inc(step, 1)
                dve.wait_ge(rstd_step, 2 * (q + 1))
                for j, (_, rows) in enumerate(TILES):
                    nc.vector.tensor_scalar(dst[0:rows, j, :], src[0:rows, j, :], mv[0:rows, j, 0:1],
                                            rstd[0:rows, j:j + 1], ALU.subtract, ALU.mult).then_inc(step, 1)

            def pre_norm(q, par):
                dve.wait_ge(h_ld[par], (q - par) * 24 + 48)
                layer_norm(q, ln1_step, ln1_rstd_step, h_in[:, par], ln1_stats, ln1_mv, ln1_rstd, xn)

            def pre_k(q, par):
                for m in range(QM):
                    n = PRE_QK + QM + m
                    dve.wait_ge(pre_full[n % 2], pre_count(q, n))
                    nc.vector.tensor_copy(k_sb[:, par, m, :], pre_ps[n % 2][:, 0:NT]).then_inc(pre_evac[n % 2], 1)

            def pre_v(q, par, img):
                n = PRE_V + 2 * img + 1
                dve.wait_ge(pre_full[n % 2], pre_count(q, n))
                nc.vector.tensor_copy(v_sb[0:T, par, img, HH:H, :].rearrange("p h v -> p (h v)"),
                                      pre_ps[n % 2][0:T, 0:HH * VD]).then_inc(pre_evac[n % 2], 1)

            def pre_u(q):
                for half in range(2):
                    n = PRE_U + half
                    dve.wait_ge(pre_full[n % 2], pre_count(q, n))
                    for j in range(J):
                        count = len(range(j, T, J))
                        rows = slice(j * RF, (j + 1) * RF)
                        heads = slice(half * HH, (half + 1) * HH)
                        ps = pre_ps[n % 2][rows, 0:HH * G * RG].rearrange("p (h i g) -> p h i g", h=HH, i=G)
                        bias = u_bias[rows, heads].unsqueeze(2).unsqueeze(3).to_broadcast([RF, HH, G, count])
                        last = nc.vector.tensor_tensor(u_diag[rows, j, heads, :, 0:count], ps[:, :, :, 0:count],
                                                       bias, ALU.add)
                    last.then_inc(pre_evac[n % 2], 1)

            def pre_rel(q, par):
                for r in range(1, RBATCHES, 2):
                    dve.wait_ge(pre_full[(PRE_REL + r) % 2], pre_count(q, PRE_REL + r))
                    for o, i in rel_copies(par, r):
                        last = nc.vector.tensor_copy(o, i)
                    last.then_inc(pre_evac[(PRE_REL + r) % 2], 1)

            def scores_add(where):
                if where is None:
                    return
                q, par, k, a = where
                img, half = divmod(k, 2)
                if k == 0:
                    for r in (RBATCHES - 2, RBATCHES - 1):
                        dve.wait_ge(pre_evac[(PRE_REL + r) % 2], pre_count(q, PRE_REL + r))
                dve.wait_ge(st_full, a + 1)
                rel = rel_sb[0:T, par].rearrange("p (h i) t -> p h i t", i=G)[:, half::2, img, :]
                nc.vector.tensor_tensor(st_sb[:, k % 2], st_ps[0:T, 0:HT].rearrange("p (h t) -> p h t", h=HH), rel,
                                        ALU.add).then_inc(st_evac, 1)

            def scores_shift(where):
                if where is None:
                    return
                a, buf = where[3], a_parity(where)
                ps = s_ps[0:T, 0:HT].rearrange("p (h t) -> p h t", h=HH)
                dve.wait_ge(s_full, a + 1)
                nc.vector.reduce_max(smax[:, buf], ps, AX.X).then_inc(max_done, 1)
                dve.wait_ge(max_done, a + 1)
                nc.vector.tensor_tensor(shifted[:, buf], ps, smax[:, buf].unsqueeze(2).to_broadcast([T, HH, T]),
                                        ALU.subtract).then_inc(s_evac, 1)

            def prob_sums(where):
                if where is None:
                    return
                a, buf = where[3], a_parity(where)
                dve.wait_ge(exp_done, a + 1)
                nc.vector.reduce_sum(psums[:, buf], prob[:, buf], AX.X).then_inc(sum_done, 1)
                dve.wait_ge(sum_done, a + 1)
                nc.vector.reciprocal(precip[:, buf], psums[:, buf]).then_inc(recip_done, 1)

            def post_residual(q, par):
                dve.wait_ge(hbo_done, q + 1)
                for j, (_, rows) in enumerate(TILES):
                    n = POST_WO + j
                    dve.wait_ge(post_full[n % 2], post_count(q, n))
                    nc.vector.tensor_tensor(h1[0:rows, j, :], post_ps[n % 2][0:rows, 0:D], h_bo[0:rows, par, j, :],
                                            ALU.add).then_inc(post_evac[n % 2], 1)

            def post_norm(q):
                for j in range(3):
                    dve.wait_ge(post_evac[(POST_WO + j) % 2], post_count(q, POST_WO + j))
                layer_norm(q, ln2_step, ln2_rstd_step, h1, ln2_stats, ln2_mv, ln2_rstd, x2)

            def post_output(q):
                wait(dve, y_out, q * 48)
                for j, (_, rows) in enumerate(TILES):
                    n = POST_DOWN + j
                    dve.wait_ge(post_full[n % 2], post_count(q, n))
                    nc.vector.tensor_tensor(y_sb[0:rows, j, :], post_ps[n % 2][0:rows, 0:D], h1[0:rows, j, :],
                                            ALU.add).then_inc(post_evac[n % 2], 1)

            def iteration(q, par, pre, post):
                for slot in range(HALVES):
                    if slot == 3 and post:
                        post_residual(q - 1, 1 - par)
                    scores_add(lagged(q, par, slot, 0))
                    scores_shift(lagged(q, par, slot, 1))
                    if slot == 3 and post:
                        post_norm(q - 1)
                    if pre and slot == 0:
                        pre_norm(q + 1, 1 - par)
                    if pre and slot == 2:
                        pre_k(q + 1, 1 - par)
                        pre_v(q + 1, 1 - par, 0)
                    if pre and slot == 3:
                        pre_v(q + 1, 1 - par, 1)
                    if pre and slot == 4:
                        pre_v(q + 1, 1 - par, 2)
                        pre_v(q + 1, 1 - par, 3)
                    if pre and slot == 6:
                        pre_u(q + 1)
                        pre_rel(q + 1, 1 - par)
                    if post and slot == 7:
                        post_output(q - 1)
                    prob_sums(lagged(q, par, slot, 1))

            def tail(q, par):
                scores_shift(lagged(q, par, 0, 1))
                prob_sums(lagged(q, par, 0, 1))
                post_residual(q - 1, 1 - par)
                post_norm(q - 1)
                post_output(q - 1)

            dve.wait_ge(cleared, 2)
            pre_norm(0, 0)
            pre_k(0, 0)
            for img in range(G):
                pre_v(0, 0, img)
            dve.wait_ge(u_ready, 2)
            pre_u(0)
            pre_rel(0, 0)
            passes(dve, iteration, tail)


def kernel(x, cls_tok, L0_tok_W0, L0_tok_b0, L0_tok_W1, L0_tok_b1, L0_tok_W2, L0_tok_b2, L0_attn_Wq, L0_attn_Wk,
           L0_attn_Wv, L0_attn_Wrk, L0_attn_r_w_bias, L0_attn_r_r_bias, L0_attn_Wo, L0_attn_bo, L0_ffn_in_weight,
           L0_ffn_in_bias, L0_ffn_out_weight):
    import concourse.bacc as bacc
    from concourse.bass_utils import run_bass_kernel_spmd

    a = np.asarray
    p = PATCHES[0]

    def chunked(w):
        return a(w).reshape(KC, DK, -1).transpose(1, 0, 2)

    def patch_weight(w, side):
        w = a(w).reshape(side, p, side, p, CH, D).transpose(1, 3, 4, 0, 2, 5)
        return w.reshape(KC, DK, side * side, D).transpose(1, 0, 2, 3)

    pix = a(x).reshape(B, 2, 4, p, 2, 4, p, CH).transpose(3, 6, 7, 2, 5, 1, 4, 0)
    b_tok = np.stack([a(L0_tok_b0), a(L0_tok_b1), a(L0_tok_b2)])
    arrays = {
        "pix": pix.reshape(KC, DK, SUB, NB).transpose(1, 0, 2, 3),
        "cls": np.broadcast_to(a(cls_tok)[0], (B, D)),
        "w0": chunked(L0_tok_W0),
        "w1": patch_weight(L0_tok_W1, 2),
        "w2": patch_weight(L0_tok_W2, 4),
        "b_tok": np.broadcast_to(b_tok[None], (128, 3, D)),
        "w_q": chunked(L0_attn_Wq),
        "w_k": chunked(L0_attn_Wk),
        "w_v": chunked(L0_attn_Wv),
        "w_qt": a(L0_attn_Wq).reshape(D, H, KD).transpose(2, 1, 0),
        "w_rkt": a(L0_attn_Wrk).reshape(RF, H, KD).transpose(2, 1, 0),
        "rw_bias": a(L0_attn_r_w_bias).reshape(QM, 128).T,
        "rr_bias": a(L0_attn_r_r_bias).T,
        "w_o": a(L0_attn_Wo).reshape(H, VD, D).transpose(1, 0, 2),
        "b_o": np.broadcast_to(a(L0_attn_bo)[None], (128, D)),
        "w_in": chunked(a(L0_ffn_in_weight).T),
        "b_in": a(L0_ffn_in_bias).reshape(MH, 128).T,
        "w_out": a(L0_ffn_out_weight).reshape(MH, 128, D).transpose(1, 0, 2),
        "ident": np.eye(128, dtype=np.float32),
        "windows": positional_windows(),
    }
    nc = bacc.Bacc("TRN2", target_bir_lowering=False, num_devices=1)
    feeds, ins = {}, {}
    for name, value in arrays.items():
        value = np.ascontiguousarray(value)
        feeds[f"in_{name}"] = value
        ins[name] = nc.dram_tensor(f"in_{name}", value.shape, mybir.dt.from_np(value.dtype), kind="ExternalInput").ap()
    out = nc.dram_tensor("out_h", (B, T, D), F32, kind="ExternalOutput").ap()
    build(nc, ins, out)
    result = run_bass_kernel_spmd(nc, [feeds], core_ids=[0])
    return result.results[0]["out_h"]
```

```python
from contextlib import ExitStack

import numpy as np

import concourse.bass as bass
from concourse import mybir

F32 = mybir.dt.float32
F32R = mybir.dt.float32r
ALU = mybir.AluOpType
ACT = mybir.ActivationFunctionType
AX = mybir.AxisListType

B, IMG, CH = 32, 64, 3
D = 192
H, KD, VD, RF = 8, 64, 96, 32
HID = 768
PATCHES = (8, 16, 32)
GRIDS = tuple(IMG // p for p in PATCHES)
FIRST_TOKEN = (1, 1 + GRIDS[0] ** 2, 1 + GRIDS[0] ** 2 + GRIDS[1] ** 2)
T = FIRST_TOKEN[2] + GRIDS[2] ** 2
EPS = 1e-5
QSCALE = KD ** -0.5

KC = 2
DK = D // KC
G = 4
NQ = B // G
NT = G * T
TILE = 114
TILES = [(j * TILE, min(TILE, NT - j * TILE)) for j in range(-(-NT // TILE))]
HH = H // 2
HALVES = 2 * G
HT = HH * T
J = 4
RG = -(-T // J)
RWIN = 2 * T - 1
RBATCH = 4
RBATCHES = -(-RG // RBATCH)
HB = H * G
QM = H * KD // 128
MH = HID // 128
PIX = PATCHES[0] ** 2 * CH
SUB = (PATCHES[2] // PATCHES[0]) ** 2
NB = B * GRIDS[2] ** 2

KA, KB = 128, D - 128
WQ, WK, WV, WIN = 0, H * KD, 2 * H * KD, 2 * H * KD + H * VD
WCOLS = WIN + HID
RING = 4

PRE_XT, PRE_QK, PRE_U, PRE_REL = 0, 2, 2 + 2 * QM, 4 + 2 * QM
PRE_V = PRE_REL + RBATCHES
PRE_USES = PRE_V + 2 * G
POST_WO, POST_XT, POST_UP, POST_DOWN = 0, 3, 5, 5 + MH
POST_USES = POST_DOWN + 3

LAG_SCORES, LAG_PROBS, LAG_VALUES = 1, 3, 4
PLAN = {
    (0, 0): [("v", 0), ("norm1", 0)],
    (0, 1): [("v", 1)],
    (1, 0): [("v", 2)],
    (1, 1): [("v", 3)],
    (1, 2): [("xt", 0)],
    (2, 0): [("qk", 0), ("qk", 1)],
    (2, 1): [("qk", 2), ("qk", 3)],
    (2, 2): [("qk", 4), ("qk", 5)],
    (3, 0): [("qk", 6), ("qk", 7)],
    (3, 1): [("u", 0), ("u", 1)],
    (3, 2): [("rel", 0), ("rel", 1)],
    (4, 0): [("wo", 0)],
    (4, 1): [("wo", 1)],
    (4, 2): [("wo", 2), ("norm2", 0)],
    (5, 0): [("rel", 2), ("rel", 3)],
    (5, 1): [("rel", 4), ("bias", 0)],
    (5, 2): [("rel", 5)],
    (6, 0): [("x2t", 0), ("up", 0)],
    (6, 1): [("up", 1), ("up", 2)],
    (6, 2): [("up", 3), ("up", 4), ("up", 5)],
    (7, 0): [("down", 0)],
    (7, 1): [("down", 1)],
    (7, 2): [("down", 2)],
}
OF_POST = ("wo", "norm2", "x2t", "up", "down")
assert PRE_USES % 2 == 0 and POST_USES % 2 == 0 and NB == 128


def positional_windows():
    nb = RF // 2
    rate = np.exp(np.log(T + 1) / nb).astype(np.float32)
    widths = rate ** np.arange(1, nb + 1, dtype=np.float32) - np.float32(1)
    pos = np.arange(RWIN)[None, :] - np.arange(J)[:, None] - (T - 1)
    inside = (widths[None, :, None] > np.abs(pos)[:, None, :]).astype(np.float32)
    signed = np.sign(pos)[:, None, :] * inside
    return np.concatenate([inside, signed], axis=1).reshape(J * RF, RWIN).astype(np.float32)


def build(nc, ins, out):
    with ExitStack() as ctx:
        def sb(name, shape, dtype=F32):
            return ctx.enter_context(nc.sbuf_tensor(name, shape, dtype))

        def psum(name):
            return ctx.enter_context(nc.psum_tensor(name, [128, 512], F32))

        def sem(name):
            return ctx.enter_context(nc.semaphore(name))

        b_tok = sb("b_tok", [128, 3, D])
        w_hi = sb("w_hi", [128, WCOLS], F32R)
        w_lo = sb("w_lo", [128, WCOLS], F32R)
        w_bhi = sb("w_bhi", [128, WCOLS], F32R)
        w_blo = sb("w_blo", [128, WCOLS], F32R)
        w_rkt = sb("w_rkt", [KD, H, RF])
        rw_bias = sb("rw_bias", [128, QM])
        rr_bias = sb("rr_bias", [KD, H])
        w_o = sb("w_o", [VD, H, D])
        b_o = sb("b_o", [128, D])
        b_in = sb("b_in", [128, MH])
        w_out = sb("w_out", [128, MH, D])
        ident = sb("ident", [128, 128])
        windows = sb("windows", [J * RF, RWIN])
        w_u = sb("w_u", [128, KC, H, RF])
        u_bias = sb("u_bias", [J * RF, H])

        neg_half = sb("neg_half", [128, 3])
        eps = sb("eps", [128, 3])
        spare = sb("spare", [1, 2])

        arena_v = sb("arena_v", [128, 2 * G * H * VD])
        v_sb = arena_v[:, :].rearrange("p (r i h v) -> p r i h v", r=2, i=G, h=H)
        w_tok2 = arena_v[0:DK, 0:KC * SUB * D].rearrange("p (k s d) -> p k s d", k=KC, s=SUB)
        arena_r = sb("arena_r", [128, 2 * HB * T])
        rel_sb = arena_r[:, :].rearrange("p (r n t) -> p r n t", r=2, n=HB)
        pix = arena_r[0:DK, 0:KC * SUB * NB].rearrange("p (k s n) -> p k s n", k=KC, s=SUB)
        k_sb = sb("k_sb", [128, 2, QM, NT])
        arena_k = k_sb[:, :, :, :].rearrange("p r m n -> p (r m n)")
        w_tok0 = arena_k[0:DK, 0:KC * D].rearrange("p (k d) -> p k d", k=KC)
        w_tok1 = arena_k[0:DK, KC * D:5 * KC * D].rearrange("p (k s d) -> p k s d", k=KC, s=4)
        TOK_RING = 4
        tok_sb = arena_k[:, 5 * KC * D:(5 * KC + TOK_RING) * D].rearrange("p (r d) -> p r d", r=TOK_RING)
        hid = sb("hid", [128, MH, NT])
        w_qt = hid[0:KD, :, :].rearrange("p m n -> p (m n)")[:, 0:H * D].rearrange("p (h d) -> p h d", h=H)

        h_in = sb("h_in", [128, 2, 3, D])
        h_bo = sb("h_bo", [128, 2, 3, D])
        ln1_stats = sb("ln1_stats", [128, 3, 6])
        ln1_mv = sb("ln1_mv", [128, 3, 2])
        ln1_rstd = sb("ln1_rstd", [128, 3])
        xn = sb("xn", [128, 3, D])
        xnt = sb("xnt", [128, KC, NT])
        x_hi = sb("x_hi", [128, NT], F32R)
        x_lo = sb("x_lo", [128, NT], F32R)
        x_b = sb("x_b", [128, NT], F32R)
        q_sb = sb("q_sb", [128, 2, QM, NT])
        u_diag = sb("u_diag", [J * RF, J, H, G, RG])
        st_sb = sb("st_sb", [T, 2, HH, T])
        smax = sb("smax", [T, 2, HH])
        shifted = sb("shifted", [T, 2, HH, T])
        prob = sb("prob", [T, RING, HH, T])
        psums = sb("psums", [T, RING, HH])
        precip = sb("precip", [T, RING, HH])
        probn = sb("probn", [T, RING, HH, T])
        pt_sb = sb("pt_sb", [T, RING, HH, T])
        arena_o = sb("arena_o", [128, H * NT])
        ot_sb = arena_o[0:VD, :].rearrange("p (h n) -> p h n", h=H)
        w_a_raw = arena_o[:, 0:WCOLS]
        w_b_raw = q_sb[:, :, :, :].rearrange("p r m n -> p (r m n)")[:, 0:WCOLS]
        h1 = sb("h1", [128, 3, D])
        ln2_stats = sb("ln2_stats", [128, 3, 6])
        ln2_mv = sb("ln2_mv", [128, 3, 2])
        ln2_rstd = sb("ln2_rstd", [128, 3])
        x2 = sb("x2", [128, 3, D])
        x2_hi = sb("x2_hi", [128, NT], F32R)
        x2_lo = sb("x2_lo", [128, NT], F32R)
        x2_b = sb("x2_b", [128, NT], F32R)
        y_sb = sb("y_sb", [128, 3, D])

        st_ps, s_ps, pt_ps, ot_ps = (psum(n) for n in ("st_ps", "s_ps", "pt_ps", "ot_ps"))
        pre_ps = [psum("pre_ps0"), psum("pre_ps1")]
        post_ps = [psum("post_ps0"), psum("post_ps1")]
        tok_ps = [pre_ps[0], pre_ps[1], post_ps[0], post_ps[1]]

        h_dram = nc.dram_tensor("h_scratch", (B, T, D), F32, kind="Internal").ap()
        h_rows = h_dram.rearrange("b t d -> (b t) d")
        out_rows = out.rearrange("b t d -> (b t) d")

        ld = {n: sem("ld_" + n) for n in (
            "w0", "pix", "w1", "w2", "btok", "qk", "v", "u", "rwb", "o", "in", "bin", "out", "const")}
        tok_mm = sem("tok_mm")
        tok_add = sem("tok_add")
        tok_wr = [sem(f"tok_wr{i}") for i in range(TOK_RING)]
        cls_wr = sem("cls_wr")
        cleared = sem("cleared")
        w_split = sem("w_split")
        x_split = sem("x_split")
        x2_hi_done = sem("x2_hi_done")
        u_mm = sem("u_mm")
        u_ready = sem("u_ready")
        h_ld = [sem("h_ld0"), sem("h_ld1")]
        hbo_done = sem("hbo_done")
        ln1_step = sem("ln1_step")
        ln2_step = sem("ln2_step")
        ln1_rstd_step = sem("ln1_rstd_step")
        ln2_rstd_step = sem("ln2_rstd_step")
        pre_full = [sem("pre_full0"), sem("pre_full1")]
        pre_evac = [sem("pre_evac0"), sem("pre_evac1")]
        post_full = [sem("post_full0"), sem("post_full1")]
        post_evac = [sem("post_evac0"), sem("post_evac1")]
        st_full, st_evac = sem("st_full"), sem("st_evac")
        s_full = sem("s_full")
        max_done = sem("max_done")
        s_evac = sem("s_evac")
        exp_done = sem("exp_done")
        sum_done = sem("sum_done")
        recip_done = sem("recip_done")
        probn_done = sem("probn_done")
        pt_full, pt_evac = sem("pt_full"), sem("pt_evac")
        ot_full, ot_evac = sem("ot_full"), sem("ot_evac")
        y_out = sem("y_out")

        block = ctx.enter_context(nc.Block())

        def wait(eng, s, value):
            if isinstance(value, int) and value <= 0:
                return
            eng.wait_ge(s, value)

        def pre_count(q, n):
            return q * (PRE_USES // 2) + (n // 2 + 1)

        def post_count(q, n):
            return q * (POST_USES // 2) + (n // 2 + 1)

        def lagged(q, par, slot, lag):
            if slot >= lag:
                return None if isinstance(q, int) and q == NQ else (q, par, slot - lag, q * HALVES + (slot - lag))
            if isinstance(q, int) and q == 0:
                return None
            k = slot - lag + HALVES
            return (q - 1, 1 - par, k, q * HALVES + (slot - lag))

        def a_parity(where):
            return where[2] % 2

        def ring(where):
            return where[2] % RING

        def dense(work, q, par, slot, part, pre, post):
            for kind, n in PLAN.get((slot, part), ()):
                if kind not in work:
                    continue
                if kind == "v":
                    work[kind](q, par, n)
                elif kind in OF_POST and post:
                    work[kind](q - 1, 1 - par, n)
                elif kind not in OF_POST and pre:
                    work[kind](q + 1, 1 - par, n)

        def rel_copies(par, r):
            bank = pre_ps[(PRE_REL + r) % 2]
            first = r * RBATCH
            whole = min(RBATCH, T // J - first)
            pairs = [(rel_sb[0:T, par, :, J * first:J * (first + whole)].rearrange("p n (g j) -> p n g j", j=J),
                      bank[0:T, 0:whole * J * HB].rearrange("p (g j n) -> p n g j", g=whole, j=J))]
            if first + whole < min(first + RBATCH, RG):
                js = T - J * (first + whole)
                pairs.append((rel_sb[0:T, par, :, J * (first + whole):T],
                              bank[0:T, whole * J * HB:(whole * J + js) * HB].rearrange("p (j n) -> p n j", j=js)))
            return pairs

        def passes(eng, iteration, tail):
            iteration(0, 0, pre=True, post=False)
            with eng.Fori(1, NQ - 1, 2) as q:
                iteration(q, 1, pre=True, post=True)
                iteration(q + 1, 0, pre=True, post=True)
            iteration(NQ - 1, 1, pre=False, post=True)
            tail(NQ, 0)

        @block.sync
        def _(sp):
            def load_weights(name, c0, c1):
                sp.dma_start(w_a_raw[:, c0:c1], ins["w_a"][:, c0:c1]).then_inc(ld[name], 16)
                sp.dma_start(w_b_raw[:, c0:c1], ins["w_b"][:, c0:c1]).then_inc(ld[name], 16)

            sp.dma_start(w_tok0, ins["w0"]).then_inc(ld["w0"], 16)
            sp.dma_start(pix[:, 0], ins["pix"][:, 0]).then_inc(ld["pix"], 16)
            sp.dma_start(pix[:, 1], ins["pix"][:, 1]).then_inc(ld["pix"], 16)
            sp.dma_start(b_tok[:, :, :], ins["b_tok"]).then_inc(ld["btok"], 16)
            sp.dma_start(w_tok1, ins["w1"]).then_inc(ld["w1"], 16)
            sp.dma_start(w_tok2, ins["w2"]).then_inc(ld["w2"], 16)
            sp.dma_start(w_qt, ins["w_qt"]).then_inc(ld["u"], 16)
            sp.dma_start(w_rkt[:, :, :], ins["w_rkt"]).then_inc(ld["u"], 16)
            sp.dma_start(rr_bias[:, :], ins["rr_bias"]).then_inc(ld["u"], 16)
            sp.dma_start(ident[:, :], ins["ident"]).then_inc(ld["const"], 16)
            sp.dma_start(windows[:, :], ins["windows"]).then_inc(ld["const"], 16)
            sp.dma_start(b_o[:, :], ins["b_o"]).then_inc(ld["const"], 16)
            load_weights("qk", WQ, WV)
            sp.dma_start(rw_bias[:, :], ins["rw_bias"]).then_inc(ld["rwb"], 16)
            load_weights("v", WV, WIN)
            sp.dma_start(w_o[:, :, :], ins["w_o"]).then_inc(ld["o"], 16)
            load_weights("in", WIN, WCOLS)
            sp.dma_start(b_in[:, :], ins["b_in"]).then_inc(ld["bin"], 16)
            sp.dma_start(w_out[:, :, :], ins["w_out"]).then_inc(ld["out"], 16)

            def load_quad(q, par):
                wait(sp, ln1_step, (q - 1) * 9)
                wait(sp, hbo_done, q - 1)
                for j, (t0, rows) in enumerate(TILES):
                    sp.dma_start(h_in[0:rows, par, j, :],
                                 h_rows[bass.ds(q * NT + t0, rows), :]).then_inc(h_ld[par], 16)

            def store_quad(q):
                for j, (t0, rows) in enumerate(TILES):
                    sp.wait_ge(post_evac[(POST_DOWN + j) % 2], post_count(q, POST_DOWN + j))
                    sp.dma_start(out_rows[bass.ds(q * NT + t0, rows), :],
                                 y_sb[0:rows, j, :]).then_inc(y_out, 16)

            for i in range(TOK_RING):
                tiles = len(range(i, SUB + 4 + 1, TOK_RING))
                sp.wait_ge(tok_wr[i], 16 * tiles * 2)
            sp.wait_ge(cls_wr, 16)
            sp.wait_ge(cleared, 1)
            load_quad(0, 0)
            load_quad(1, 1)
            load_quad(2, 0)
            with sp.Fori(1, NQ - 3, 1 + 1) as q:
                store_quad(q - 1)
                load_quad(q + 2, 1)
                store_quad(q)
                load_quad(q + 3, 0)
            for q in range(NQ - 3, NQ + 1):
                store_quad(q - 1)
                if q + 2 < NQ:
                    load_quad(q + 2, (q + 2) % 2)
            sp.wait_ge(y_out, NQ * 3 * 16)

        @block.gpsimd
        def _(pool):
            pool.dma_start(h_dram[:, 0, :], ins["cls"]).then_inc(cls_wr, 16)
            nc.gpsimd.memset(neg_half[:, :], -0.5)
            nc.gpsimd.memset(eps[:, :], EPS)
            for buf in (h_in, h_bo, ln1_mv, ln2_mv):
                nc.gpsimd.memset(buf[tuple(slice(None) for _ in buf.shape)], 0.0)
            nc.gpsimd.memset(h1[:, :, :], 0.0).then_inc(cleared, 1)
            nc.gpsimd.memset(xnt[:, 1, :], 0.0)
            nc.gpsimd.memset(w_u[:, 1], 0.0).then_inc(cleared, 1)
            nc.gpsimd.memset(u_diag[:, :, :, :, :], 0.0).then_inc(cleared, 1)

            step = 0
            for name, c0, c1 in (("qk", WQ, WV), ("v", WV, WIN), ("in", WIN, WCOLS)):
                pool.wait_ge(ld[name], 32)
                nc.gpsimd.tensor_copy(w_hi[:, c0:c1], w_a_raw[:, c0:c1]).then_inc(w_split, 1)
                nc.gpsimd.tensor_copy(w_bhi[:, c0:c1], w_b_raw[:, c0:c1]).then_inc(w_split, 1)
                pool.wait_ge(w_split, step + 1)
                nc.gpsimd.tensor_tensor(w_lo[:, c0:c1], w_a_raw[:, c0:c1], w_hi[:, c0:c1].bitcast(F32),
                                        ALU.subtract).then_inc(w_split, 1)
                pool.wait_ge(w_split, step + 2)
                nc.gpsimd.tensor_tensor(w_blo[:, c0:c1], w_b_raw[:, c0:c1], w_bhi[:, c0:c1].bitcast(F32),
                                        ALU.subtract).then_inc(w_split, 1)
                step += 4

            def bias(q, par, _):
                pool.wait_ge(h_ld[par], (q - par) * 24 + 48)
                wait(pool, post_evac[0], post_count(q - 2, POST_WO + 2))
                wait(pool, post_evac[1], post_count(q - 2, POST_WO + 1))
                nc.gpsimd.tensor_tensor(h_bo[:, par], h_in[:, par],
                                        b_o[:, :].unsqueeze(1).to_broadcast([128, 3, D]),
                                        ALU.add).then_inc(hbo_done, 1)

            def rstd(q, step, rstd_step, mv, out):
                pool.wait_ge(step, q * 9 + 6)
                nc.gpsimd.tensor_tensor(out[:, :], mv[:, :, 1], eps[:, :], ALU.add).then_inc(rstd_step, 1)
                pool.wait_ge(rstd_step, 2 * q + 1)
                nc.gpsimd.tensor_tensor(out[:, :], out[:, :], neg_half[:, :], ALU.pow).then_inc(rstd_step, 1)

            def normalize(where):
                if where is None:
                    return
                a, buf = where[3], ring(where)
                pool.wait_ge(recip_done, a + 1)
                wait(pool, pt_full, a - RING + 1)
                nc.gpsimd.tensor_tensor(probn[:, buf], prob[:, buf],
                                        precip[:, buf].unsqueeze(2).to_broadcast([T, HH, T]),
                                        ALU.mult).then_inc(probn_done, 1)

            work = {
                "norm1": lambda q, par, _: rstd(q, ln1_step, ln1_rstd_step, ln1_mv, ln1_rstd),
                "norm2": lambda q, par, _: rstd(q, ln2_step, ln2_rstd_step, ln2_mv, ln2_rstd),
                "bias": bias,
            }

            def iteration(q, par, pre, post):
                for slot in range(HALVES):
                    dense(work, q, par, slot, 0, pre, post)
                    dense(work, q, par, slot, 1, pre, post)
                    normalize(lagged(q, par, slot, LAG_SCORES))
                    dense(work, q, par, slot, 2, pre, post)

            def tail(q, par):
                normalize(lagged(q, par, 0, LAG_SCORES))
                work["norm2"](q - 1, 1 - par, 0)

            pool.wait_ge(ld["const"], 48)
            bias(0, 0, 0)
            work["norm1"](0, 0, 0)
            passes(pool, iteration, tail)

        @block.tensor
        def _(pe):
            def tok_tile(i, products):
                bank = tok_ps[i % 4]
                wait(pe, tok_add, i - 3)
                for n, (lhs, rhs) in enumerate(products):
                    last = nc.tensor.matmul(bank[:, 0:D], lhs, rhs, start=(n == 0),
                                            stop=(n == len(products) - 1))
                last.then_inc(tok_mm, 1)

            pe.wait_ge(ld["w0"], 16)
            pe.wait_ge(ld["pix"], 32)
            for s in range(SUB):
                tok_tile(s, [(pix[:, k, s, :], w_tok0[:, k, :]) for k in range(KC)])
            pe.wait_ge(ld["w1"], 16)
            for t in range(4):
                yb, xb = divmod(t, 2)
                tok_tile(SUB + t, [(pix[:, k, (2 * yb + ya) * 4 + 2 * xb + xa, :], w_tok1[:, k, 2 * ya + xa, :])
                                   for ya in range(2) for xa in range(2) for k in range(KC)])
            pe.wait_ge(ld["w2"], 16)
            tok_tile(SUB + 4, [(pix[:, k, s, :], w_tok2[:, k, s, :]) for s in range(SUB) for k in range(KC)])

            pe.wait_ge(ld["u"], 48)
            for h in range(H):
                for k, (row, rows) in enumerate(((0, KA), (KA, KB))):
                    last = nc.tensor.matmul(st_ps[0:rows, (k * H + h) * RF:(k * H + h + 1) * RF],
                                            w_qt[:, h, row:row + rows], w_rkt[:, h, :], start=True, stop=True)
            for j in range(J):
                for h in range(H):
                    last = nc.tensor.matmul(s_ps[j * RF:(j + 1) * RF, h:h + 1], w_rkt[:, h, :],
                                            rr_bias[:, h:h + 1], start=True, stop=True)
            last.then_inc(u_mm, 1)

            def pre_use(q, n):
                wait(pe, pre_evac[n % 2], q * (PRE_USES // 2) + n // 2)
                return pre_ps[n % 2]

            def xt(q, par, _):
                pe.wait_ge(ln1_step, (q + 1) * 9)
                banks = [pre_use(q, PRE_XT + k) for k in range(KC)]
                for k, (row, rows) in enumerate(((0, KA), (KA, KB))):
                    bank = banks[k]
                    for j, (t0, tokens) in enumerate(TILES):
                        last = nc.tensor.transpose(bank[0:rows, t0:t0 + tokens], xn[0:tokens, j, row:row + rows],
                                                   ident[0:tokens, 0:tokens])
                    last.then_inc(pre_full[(PRE_XT + k) % 2], 1)

            def qk(q, par, m):
                n = PRE_QK + m
                c = WQ + m * 128
                bank = pre_use(q, n)
                if m == 0:
                    pe.wait_ge(x_split, (q + 1) * 4)
                passes_of = [(w_hi, x_hi), (w_hi, x_lo), (w_lo, x_hi), (w_bhi, x_b), (w_blo, x_b)]
                for i, (w, x) in enumerate(passes_of):
                    last = nc.tensor.matmul(bank[:, 0:NT], w[:, c:c + 128], x[:, :], start=(i == 0),
                                            stop=(i == len(passes_of) - 1))
                last.then_inc(pre_full[n % 2], 1)

            def v(q, par, img):
                tok = slice(img * T, (img + 1) * T)
                passes_of = [(x_hi, w_hi), (x_hi, w_lo), (x_lo, w_hi), (x_b, w_bhi), (x_b, w_blo)]
                for half in range(2):
                    n = PRE_V + 2 * img + half
                    bank = pre_use(q, n)
                    c = WV + half * HH * VD
                    for i, (x, w) in enumerate(passes_of):
                        last = nc.tensor.matmul(bank[0:T, 0:HH * VD], x[:, tok], w[:, c:c + HH * VD],
                                                start=(i == 0), stop=(i == len(passes_of) - 1))
                    last.then_inc(pre_full[n % 2], 1)

            def u(q, par, half):
                n = PRE_U + half
                bank = pre_use(q, n)
                for h in range(HH):
                    for j in range(J):
                        count = len(range(j, T, J))
                        o = bank[j * RF:(j + 1) * RF, h * G * RG:(h + 1) * G * RG]
                        o = o.rearrange("p (i g) -> p i g", i=G)[:, :, 0:count]
                        for k in range(KC):
                            x = xnt[:, k, :].rearrange("p (i t) -> p i t", i=G)[:, :, j::J]
                            last = nc.tensor.matmul(o, w_u[:, k, half * HH + h, :], x, start=(k == 0),
                                                    stop=(k == KC - 1))
                last.then_inc(pre_full[n % 2], 1)

            def rel(q, par, r):
                n = PRE_REL + r
                bank = pre_use(q, n)
                if r == 0:
                    for half in range(2):
                        pe.wait_ge(pre_evac[(PRE_U + half) % 2], pre_count(q, PRE_U + half))
                for g in range(r * RBATCH, min((r + 1) * RBATCH, RG)):
                    js = min(J, T - g * J)
                    c = (g - r * RBATCH) * J * HB
                    last = nc.tensor.matmul(bank[0:T, c:c + js * HB], windows[:, T - 1 - J * g:2 * T - 1 - J * g],
                                            u_diag[:, 0:js, :, :, g].rearrange("p j h i -> p j (h i)"),
                                            start=True, stop=True)
                last.then_inc(pre_full[n % 2], 1)

            def content(where):
                if where is None:
                    return
                q, par, k, a = where
                img, half = divmod(k, 2)
                if k == 0:
                    for m in (2 * QM - 2, 2 * QM - 1):
                        pe.wait_ge(pre_evac[(PRE_QK + m) % 2], pre_count(q, PRE_QK + m))
                wait(pe, st_evac, a)
                for hh in range(HH):
                    p = KD * half
                    tok = slice(img * T, (img + 1) * T)
                    last = nc.tensor.matmul(st_ps[0:T, hh * T:(hh + 1) * T], k_sb[p:p + KD, par, hh, tok],
                                            q_sb[p:p + KD, par, hh, tok], start=True, stop=True)
                last.then_inc(st_full, 1)

            def scores_transpose(where):
                if where is None:
                    return
                a = where[3]
                pe.wait_ge(st_evac, a + 1)
                wait(pe, s_evac, a)
                for hh in range(HH):
                    last = nc.tensor.transpose(s_ps[0:T, hh * T:(hh + 1) * T], st_sb[:, a_parity(where), hh, :], ident[0:T, 0:T])
                last.then_inc(s_full, 1)

            def probs_transpose(where):
                if where is None:
                    return
                a, buf = where[3], ring(where)
                pe.wait_ge(probn_done, a + 1)
                wait(pe, pt_evac, a)
                for hh in range(HH):
                    last = nc.tensor.transpose(pt_ps[0:T, hh * T:(hh + 1) * T], probn[:, buf, hh, :], ident[0:T, 0:T])
                last.then_inc(pt_full, 1)

            def weighted_values(where):
                if where is None:
                    return
                q, par, k, a = where
                img, half = divmod(k, 2)
                if half == 0:
                    for n in (PRE_V + 2 * img, PRE_V + 2 * img + 1):
                        pe.wait_ge(pre_evac[n % 2], pre_count(q, n))
                pe.wait_ge(pt_evac, a + 1)
                wait(pe, ot_evac, a)
                for hh in range(HH):
                    last = nc.tensor.matmul(ot_ps[0:VD, hh * T:(hh + 1) * T], v_sb[0:T, par, img, 2 * hh + half, :],
                                            pt_sb[:, ring(where), hh, :], start=True, stop=True)
                last.then_inc(ot_full, 1)

            def post_use(q, n):
                wait(pe, post_evac[n % 2], q * (POST_USES // 2) + n // 2)
                return post_ps[n % 2]

            def wo(q, par, j):
                t0, rows = TILES[j]
                n = POST_WO + j
                bank = post_use(q, n)
                if j == 0:
                    pe.wait_ge(ot_evac, (q + 1) * HALVES)
                for h in range(H):
                    last = nc.tensor.matmul(bank[0:rows, 0:D], ot_sb[:, h, t0:t0 + rows], w_o[:, h, :],
                                            start=(h == 0), stop=(h == H - 1))
                last.then_inc(post_full[n % 2], 1)

            def x2t(q, par, _):
                pe.wait_ge(ln2_step, (q + 1) * 9)
                banks = [post_use(q, POST_XT + k) for k in range(KC)]
                for k, (row, rows) in enumerate(((0, KA), (KA, KB))):
                    n = POST_XT + k
                    bank = banks[k]
                    for j, (t0, tokens) in enumerate(TILES):
                        last = nc.tensor.transpose(bank[0:rows, t0:t0 + tokens], x2[0:tokens, j, row:row + rows],
                                                   ident[0:tokens, 0:tokens])
                    last.then_inc(post_full[n % 2], 1)

            def up(q, par, m):
                n = POST_UP + m
                c = WIN + m * 128
                bank = post_use(q, n)
                if m == 0:
                    for k in range(KC):
                        pe.wait_ge(post_evac[(POST_XT + k) % 2], post_count(q, POST_XT + k))
                passes_of = [(w_hi, x2_hi), (w_hi, x2_lo), (w_lo, x2_hi), (w_bhi, x2_b), (w_blo, x2_b)]
                for i, (w, x) in enumerate(passes_of):
                    last = nc.tensor.matmul(bank[:, 0:NT], w[:, c:c + 128], x[:, :], start=(i == 0),
                                            stop=(i == len(passes_of) - 1))
                last.then_inc(post_full[n % 2], 1)

            def down(q, par, j):
                t0, rows = TILES[j]
                n = POST_DOWN + j
                bank = post_use(q, n)
                if j == 0:
                    for m in (MH - 2, MH - 1):
                        pe.wait_ge(post_evac[(POST_UP + m) % 2], post_count(q, POST_UP + m))
                for m in range(MH):
                    last = nc.tensor.matmul(bank[0:rows, 0:D], hid[:, m, t0:t0 + rows], w_out[:, m, :],
                                            start=(m == 0), stop=(m == MH - 1))
                last.then_inc(post_full[n % 2], 1)

            work = {"xt": xt, "qk": qk, "v": v, "u": u, "rel": rel, "wo": wo, "x2t": x2t, "up": up, "down": down}

            def iteration(q, par, pre, post):
                for slot in range(HALVES):
                    content(lagged(q, par, slot, 0))
                    dense(work, q, par, slot, 0, pre, post)
                    scores_transpose(lagged(q, par, slot, LAG_SCORES))
                    dense(work, q, par, slot, 1, pre, post)
                    probs_transpose(lagged(q, par, slot, LAG_PROBS))
                    dense(work, q, par, slot, 2, pre, post)
                    weighted_values(lagged(q, par, slot, LAG_VALUES))

            def tail(q, par):
                for slot in range(LAG_VALUES):
                    if slot < LAG_SCORES:
                        scores_transpose(lagged(q, par, slot, LAG_SCORES))
                    if slot < LAG_PROBS:
                        probs_transpose(lagged(q, par, slot, LAG_PROBS))
                    weighted_values(lagged(q, par, slot, LAG_VALUES))
                for slot in range(HALVES):
                    for part in range(3):
                        dense({k: work[k] for k in OF_POST if k in work}, q, par, slot, part, False, True)

            pe.wait_ge(ld["const"], 48)
            xt(0, 0, 0)
            pe.wait_ge(w_split, 4)
            for m in range(2 * QM):
                qk(0, 0, m)
            pe.wait_ge(u_ready, 2)
            for half in range(2):
                u(0, 0, half)
            for r in range(RBATCHES):
                rel(0, 0, r)
            pe.wait_ge(w_split, 12)
            for name, count in (("o", 16), ("out", 16)):
                pe.wait_ge(ld[name], count)
            passes(pe, iteration, tail)

        @block.scalar
        def _(act):
            def xt(q, par, _):
                for k, rows in enumerate((KA, KB)):
                    n = PRE_XT + k
                    act.wait_ge(pre_full[n % 2], pre_count(q, n))
                    nc.scalar.copy(xnt[0:rows, k, :], pre_ps[n % 2][0:rows, 0:NT]).then_inc(pre_evac[n % 2], 1)

            def qk(q, par, m):
                if m >= QM:
                    return
                n = PRE_QK + m
                act.wait_ge(pre_full[n % 2], pre_count(q, n))
                nc.scalar.activation(q_sb[:, par, m, :], pre_ps[n % 2][:, 0:NT], ACT.Identity,
                                     bias=rw_bias[:, m:m + 1], scale=QSCALE).then_inc(pre_evac[n % 2], 1)

            def v(q, par, img):
                n = PRE_V + 2 * img
                act.wait_ge(pre_full[n % 2], pre_count(q, n))
                nc.scalar.copy(v_sb[0:T, par, img, 0:HH, :],
                               pre_ps[n % 2][0:T, 0:HH * VD]).then_inc(pre_evac[n % 2], 1)

            def rel(q, par, r):
                if r % 2:
                    return
                act.wait_ge(pre_full[(PRE_REL + r) % 2], pre_count(q, PRE_REL + r))
                for o, i in rel_copies(par, r):
                    last = nc.scalar.copy(o, i)
                last.then_inc(pre_evac[(PRE_REL + r) % 2], 1)

            def exponentials(where):
                if where is None:
                    return
                a = where[3]
                act.wait_ge(s_evac, a + 1)
                wait(act, probn_done, a - RING + 1)
                nc.scalar.activation(prob[:, ring(where)], shifted[:, a_parity(where)],
                                     ACT.Exp).then_inc(exp_done, 1)

            def probs_copy(where):
                if where is None:
                    return
                a, buf = where[3], ring(where)
                act.wait_ge(pt_full, a + 1)
                wait(act, ot_full, a - RING + 1)
                nc.scalar.copy(pt_sb[:, buf], pt_ps[0:T, 0:HT]).then_inc(pt_evac, 1)

            def outputs_copy(where):
                if where is None:
                    return
                _, _, k, a = where
                img, half = divmod(k, 2)
                act.wait_ge(ot_full, a + 1)
                nc.scalar.copy(ot_sb[:, half::2, img * T:(img + 1) * T],
                               ot_ps[0:VD, 0:HT].rearrange("p (h t) -> p h t", h=HH)).then_inc(ot_evac, 1)

            def x2t(q, par, _):
                for k, (rows, dst) in enumerate(((KA, x2_hi), (KB, x2_b))):
                    n = POST_XT + k
                    act.wait_ge(post_full[n % 2], post_count(q, n))
                    nc.scalar.copy(dst[0:rows, :], post_ps[n % 2][0:rows, 0:NT]).then_inc(x2_hi_done, 1)

            def up(q, par, m):
                n = POST_UP + m
                act.wait_ge(post_full[n % 2], post_count(q, n))
                nc.scalar.activation(hid[:, m, :], post_ps[n % 2][:, 0:NT], ACT.Gelu,
                                     bias=b_in[:, m:m + 1]).then_inc(post_evac[n % 2], 1)

            work = {"xt": xt, "qk": qk, "v": v, "rel": rel, "x2t": x2t, "up": up}

            def iteration(q, par, pre, post):
                for slot in range(HALVES):
                    dense(work, q, par, slot, 0, pre, post)
                    exponentials(lagged(q, par, slot, LAG_SCORES))
                    dense(work, q, par, slot, 1, pre, post)
                    probs_copy(lagged(q, par, slot, LAG_PROBS))
                    dense(work, q, par, slot, 2, pre, post)
                    outputs_copy(lagged(q, par, slot, LAG_VALUES))

            def tail(q, par):
                for slot in range(LAG_VALUES):
                    if slot < LAG_SCORES:
                        exponentials(lagged(q, par, slot, LAG_SCORES))
                    if slot < LAG_PROBS:
                        probs_copy(lagged(q, par, slot, LAG_PROBS))
                    outputs_copy(lagged(q, par, slot, LAG_VALUES))
                x2t(q - 1, 1 - par, 0)
                for m in range(MH):
                    up(q - 1, 1 - par, m)

            for i in range(SUB + 5):
                act.wait_ge(tok_add, i + 1)
                scale, first = (0, 0) if i < SUB else (1, SUB) if i < SUB + 4 else (2, SUB + 4)
                side = GRIDS[scale] // GRIDS[2]
                ys, xs = divmod(i - first, side)
                rows = h_dram[:, FIRST_TOKEN[scale]:FIRST_TOKEN[scale] + GRIDS[scale] ** 2, :]
                rows = rows.rearrange("b (Y y X x) d -> y x Y X b d", Y=2, X=2, y=side)[ys, xs]
                for Y in range(2):
                    act.dma_start(rows[Y],
                                   tok_sb[64 * Y:64 * Y + 64, i % TOK_RING, :]).then_inc(tok_wr[i % TOK_RING], 16)

            xt(0, 0, 0)
            act.wait_ge(ld["rwb"], 16)
            for m in range(QM):
                qk(0, 0, m)
            for r in range(RBATCHES):
                rel(0, 0, r)
            act.wait_ge(ld["bin"], 16)
            passes(act, iteration, tail)

        @block.vector
        def _(dve):
            dve.wait_ge(ld["btok"], 16)
            for i in range(SUB + 5):
                scale = 0 if i < SUB else 1 if i < SUB + 4 else 2
                dve.wait_ge(tok_mm, i + 1)
                wait(dve, tok_wr[i % TOK_RING], 32 * (i // TOK_RING))
                nc.vector.tensor_tensor(tok_sb[:, i % TOK_RING, :], tok_ps[i % 4][:, 0:D], b_tok[:, scale, :],
                                        ALU.add).then_inc(tok_add, 1)
            dve.wait_ge(u_mm, 1)
            dve.wait_ge(cleared, 2)
            for k, rows in enumerate((KA, KB)):
                last = nc.vector.tensor_scalar(w_u[0:rows, k, :, :].rearrange("p h f -> p (h f)"),
                                               st_ps[0:rows, k * H * RF:(k + 1) * H * RF], QSCALE, None, ALU.mult)
            last.then_inc(u_ready, 1)
            nc.vector.tensor_copy(u_bias[:, :], s_ps[:, 0:H]).then_inc(u_ready, 1)

            def layer_norm(q, step, rstd_step, src, stats, mv, rstd, dst):
                base = q * 9
                for j, (_, rows) in enumerate(TILES):
                    nc.vector.bn_stats(stats[0:rows, j, :], src[0:rows, j, :]).then_inc(step, 1)
                dve.wait_ge(step, base + 3)
                nc.vector.memset(spare[:, :], 0.0)
                for j, (_, rows) in enumerate(TILES):
                    nc.vector.bn_aggr(mv[0:rows, j, :], stats[0:rows, j, :]).then_inc(step, 1)
                dve.wait_ge(rstd_step, 2 * (q + 1))
                for j, (_, rows) in enumerate(TILES):
                    nc.vector.tensor_scalar(dst[0:rows, j, :], src[0:rows, j, :], mv[0:rows, j, 0:1],
                                            rstd[0:rows, j:j + 1], ALU.subtract, ALU.mult).then_inc(step, 1)

            def norm1(q, par, _):
                dve.wait_ge(h_ld[par], (q - par) * 24 + 48)
                layer_norm(q, ln1_step, ln1_rstd_step, h_in[:, par], ln1_stats, ln1_mv, ln1_rstd, xn)

            def xt(q, par, _):
                for k, (rows, dst) in enumerate(((KA, x_hi), (KB, x_b))):
                    dve.wait_ge(pre_evac[(PRE_XT + k) % 2], pre_count(q, PRE_XT + k))
                    nc.vector.tensor_copy(dst[0:rows, :], xnt[0:rows, k, :]).then_inc(x_split, 1)
                dve.wait_ge(x_split, q * 4 + 1)
                nc.vector.tensor_tensor(x_lo[:, :], xnt[:, 0, :], x_hi[:, :].bitcast(F32),
                                        ALU.subtract).then_inc(x_split, 1)
                dve.wait_ge(x_split, q * 4 + 2)
                nc.vector.tensor_tensor(x_b[KB:2 * KB, :], xnt[0:KB, 1, :], x_b[0:KB, :].bitcast(F32),
                                        ALU.subtract).then_inc(x_split, 1)

            def qk(q, par, m):
                if m < QM:
                    return
                n = PRE_QK + m
                dve.wait_ge(pre_full[n % 2], pre_count(q, n))
                nc.vector.tensor_copy(k_sb[:, par, m - QM, :], pre_ps[n % 2][:, 0:NT]).then_inc(pre_evac[n % 2], 1)

            def v(q, par, img):
                n = PRE_V + 2 * img + 1
                dve.wait_ge(pre_full[n % 2], pre_count(q, n))
                nc.vector.tensor_copy(v_sb[0:T, par, img, HH:H, :].rearrange("p h v -> p (h v)"),
                                      pre_ps[n % 2][0:T, 0:HH * VD]).then_inc(pre_evac[n % 2], 1)

            def u(q, par, half):
                n = PRE_U + half
                dve.wait_ge(pre_full[n % 2], pre_count(q, n))
                for j in range(J):
                    count = len(range(j, T, J))
                    rows = slice(j * RF, (j + 1) * RF)
                    heads = slice(half * HH, (half + 1) * HH)
                    ps = pre_ps[n % 2][rows, 0:HH * G * RG].rearrange("p (h i g) -> p h i g", h=HH, i=G)
                    by_head = u_bias[rows, heads].unsqueeze(2).unsqueeze(3).to_broadcast([RF, HH, G, count])
                    last = nc.vector.tensor_tensor(u_diag[rows, j, heads, :, 0:count], ps[:, :, :, 0:count],
                                                   by_head, ALU.add)
                last.then_inc(pre_evac[n % 2], 1)

            def rel(q, par, r):
                if r % 2 == 0:
                    return
                dve.wait_ge(pre_full[(PRE_REL + r) % 2], pre_count(q, PRE_REL + r))
                for o, i in rel_copies(par, r):
                    last = nc.vector.tensor_copy(o, i)
                last.then_inc(pre_evac[(PRE_REL + r) % 2], 1)

            def scores_add(where):
                if where is None:
                    return
                q, par, k, a = where
                img, half = divmod(k, 2)
                if k == 0:
                    for r in (RBATCHES - 2, RBATCHES - 1):
                        dve.wait_ge(pre_evac[(PRE_REL + r) % 2], pre_count(q, PRE_REL + r))
                dve.wait_ge(st_full, a + 1)
                rel = rel_sb[0:T, par].rearrange("p (h i) t -> p h i t", i=G)[:, half::2, img, :]
                nc.vector.tensor_tensor(st_sb[:, k % 2], st_ps[0:T, 0:HT].rearrange("p (h t) -> p h t", h=HH), rel,
                                        ALU.add).then_inc(st_evac, 1)

            def scores_shift(where):
                if where is None:
                    return
                a, buf = where[3], a_parity(where)
                ps = s_ps[0:T, 0:HT].rearrange("p (h t) -> p h t", h=HH)
                dve.wait_ge(s_full, a + 1)
                nc.vector.reduce_max(smax[:, buf], ps, AX.X).then_inc(max_done, 1)
                dve.wait_ge(max_done, a + 1)
                nc.vector.tensor_tensor(shifted[:, buf], ps, smax[:, buf].unsqueeze(2).to_broadcast([T, HH, T]),
                                        ALU.subtract).then_inc(s_evac, 1)

            def prob_sums(where):
                if where is None:
                    return
                a, buf = where[3], ring(where)
                dve.wait_ge(exp_done, a + 1)
                nc.vector.reduce_sum(psums[:, buf], prob[:, buf], AX.X).then_inc(sum_done, 1)
                dve.wait_ge(sum_done, a + 1)
                nc.vector.reciprocal(precip[:, buf], psums[:, buf]).then_inc(recip_done, 1)

            def wo(q, par, j):
                rows = TILES[j][1]
                n = POST_WO + j
                if j == 0:
                    dve.wait_ge(hbo_done, q + 1)
                dve.wait_ge(post_full[n % 2], post_count(q, n))
                nc.vector.tensor_tensor(h1[0:rows, j, :], post_ps[n % 2][0:rows, 0:D], h_bo[0:rows, par, j, :],
                                        ALU.add).then_inc(post_evac[n % 2], 1)

            def norm2(q, par, _):
                for j in range(3):
                    dve.wait_ge(post_evac[(POST_WO + j) % 2], post_count(q, POST_WO + j))
                layer_norm(q, ln2_step, ln2_rstd_step, h1, ln2_stats, ln2_mv, ln2_rstd, x2)

            def x2t(q, par, _):
                for k, (src, dst) in enumerate(((x2_hi, x2_lo[:, :]), (x2_b, x2_b[KB:2 * KB, :]))):
                    n = POST_XT + k
                    rows = (KA, KB)[k]
                    dve.wait_ge(x2_hi_done, 2 * q + (k + 1))
                    nc.vector.tensor_tensor(dst, post_ps[n % 2][0:rows, 0:NT], src[0:rows, :].bitcast(F32),
                                            ALU.subtract).then_inc(post_evac[n % 2], 1)

            def down(q, par, j):
                rows = TILES[j][1]
                n = POST_DOWN + j
                if j == 0:
                    wait(dve, y_out, q * 48)
                dve.wait_ge(post_full[n % 2], post_count(q, n))
                nc.vector.tensor_tensor(y_sb[0:rows, j, :], post_ps[n % 2][0:rows, 0:D], h1[0:rows, j, :],
                                        ALU.add).then_inc(post_evac[n % 2], 1)

            work = {"norm1": norm1, "xt": xt, "qk": qk, "v": v, "u": u, "rel": rel, "wo": wo, "norm2": norm2,
                    "x2t": x2t, "down": down}

            def iteration(q, par, pre, post):
                for slot in range(HALVES):
                    scores_add(lagged(q, par, slot, 0))
                    dense(work, q, par, slot, 0, pre, post)
                    scores_shift(lagged(q, par, slot, LAG_SCORES))
                    dense(work, q, par, slot, 1, pre, post)
                    prob_sums(lagged(q, par, slot, LAG_SCORES))
                    dense(work, q, par, slot, 2, pre, post)

            def tail(q, par):
                scores_shift(lagged(q, par, 0, LAG_SCORES))
                prob_sums(lagged(q, par, 0, LAG_SCORES))
                for slot in range(HALVES):
                    for part in range(3):
                        dense({k: work[k] for k in OF_POST if k in work}, q, par, slot, part, False, True)

            dve.wait_ge(cleared, 3)
            norm1(0, 0, 0)
            xt(0, 0, 0)
            for m in range(QM, 2 * QM):
                qk(0, 0, m)
            dve.wait_ge(u_ready, 2)
            for half in range(2):
                u(0, 0, half)
            for r in range(RBATCHES):
                rel(0, 0, r)
            passes(dve, iteration, tail)


def kernel(x, cls_tok, L0_tok_W0, L0_tok_b0, L0_tok_W1, L0_tok_b1, L0_tok_W2, L0_tok_b2, L0_attn_Wq, L0_attn_Wk,
           L0_attn_Wv, L0_attn_Wrk, L0_attn_r_w_bias, L0_attn_r_r_bias, L0_attn_Wo, L0_attn_bo, L0_ffn_in_weight,
           L0_ffn_in_bias, L0_ffn_out_weight):
    import concourse.bacc as bacc
    from concourse.bass_utils import run_bass_kernel_spmd

    a = np.asarray
    p = PATCHES[0]

    def chunked(w):
        return a(w).reshape(KC, DK, -1).transpose(1, 0, 2)

    def patch_weight(w, side):
        w = a(w).reshape(side, p, side, p, CH, D).transpose(1, 3, 4, 0, 2, 5)
        return w.reshape(KC, DK, side * side, D).transpose(1, 0, 2, 3)

    pix = a(x).reshape(B, 2, 4, p, 2, 4, p, CH).transpose(3, 6, 7, 2, 5, 1, 4, 0)
    wide = np.concatenate([a(L0_attn_Wq), a(L0_attn_Wk), a(L0_attn_Wv), a(L0_ffn_in_weight).T], axis=1)
    b_tok = np.stack([a(L0_tok_b0), a(L0_tok_b1), a(L0_tok_b2)])
    arrays = {
        "pix": pix.reshape(KC, DK, SUB, NB).transpose(1, 0, 2, 3),
        "cls": np.broadcast_to(a(cls_tok)[0], (B, D)),
        "w0": chunked(L0_tok_W0),
        "w1": patch_weight(L0_tok_W1, 2),
        "w2": patch_weight(L0_tok_W2, 4),
        "b_tok": np.broadcast_to(b_tok[None], (128, 3, D)),
        "w_a": wide[0:KA],
        "w_b": np.concatenate([wide[KA:D], wide[KA:D]]),
        "w_qt": a(L0_attn_Wq).reshape(D, H, KD).transpose(2, 1, 0),
        "w_rkt": a(L0_attn_Wrk).reshape(RF, H, KD).transpose(2, 1, 0),
        "rw_bias": a(L0_attn_r_w_bias).reshape(QM, 128).T,
        "rr_bias": a(L0_attn_r_r_bias).T,
        "w_o": a(L0_attn_Wo).reshape(H, VD, D).transpose(1, 0, 2),
        "b_o": np.broadcast_to(a(L0_attn_bo)[None], (128, D)),
        "b_in": a(L0_ffn_in_bias).reshape(MH, 128).T,
        "w_out": a(L0_ffn_out_weight).reshape(MH, 128, D).transpose(1, 0, 2),
        "ident": np.eye(128, dtype=np.float32),
        "windows": positional_windows(),
    }
    nc = bacc.Bacc("TRN2", target_bir_lowering=False, num_devices=1)
    feeds, ins = {}, {}
    for name, value in arrays.items():
        value = np.ascontiguousarray(value)
        feeds[f"in_{name}"] = value
        ins[name] = nc.dram_tensor(f"in_{name}", value.shape, mybir.dt.from_np(value.dtype), kind="ExternalInput").ap()
    out = nc.dram_tensor("out_h", (B, T, D), F32, kind="ExternalOutput").ap()
    build(nc, ins, out)
    result = run_bass_kernel_spmd(nc, [feeds], core_ids=[0])
    return result.results[0]["out_h"]
```

```python
from contextlib import ExitStack

import numpy as np

import concourse.bass as bass
from concourse import mybir

F32 = mybir.dt.float32
F32R = mybir.dt.float32r
ALU = mybir.AluOpType
ACT = mybir.ActivationFunctionType
AX = mybir.AxisListType

B, IMG, CH = 32, 64, 3
D = 192
H, KD, VD, RF = 8, 64, 96, 32
OC = H * VD // 128
HID = 768
PATCHES = (8, 16, 32)
GRIDS = tuple(IMG // p for p in PATCHES)
FIRST_TOKEN = (1, 1 + GRIDS[0] ** 2, 1 + GRIDS[0] ** 2 + GRIDS[1] ** 2)
T = FIRST_TOKEN[2] + GRIDS[2] ** 2
EPS = 1e-5
QSCALE = KD ** -0.5

KC = 2
DK = D // KC
G = 4
NQ = B // G
NT = G * T
TILE = 114
TILES = [(j * TILE, min(TILE, NT - j * TILE)) for j in range(-(-NT // TILE))]
V_MOVES = [(j, slice(a - t0, b - t0), i, slice(a - i * T, b - i * T)) for j, (t0, rows) in enumerate(TILES)
           for i in range(G) for a, b in [(max(t0, i * T), min(t0 + rows, (i + 1) * T))] if a < b]
HH = H // 2
HALVES = 2 * G
HT = HH * T
J = 4
RG = -(-T // J)
RWIN = 2 * T - 1
OQ = OC // 2 * 4
RBATCH = 4
RBATCHES = -(-RG // RBATCH)
HB = H * G
QM = H * KD // 128
MH = HID // 128
PIX = PATCHES[0] ** 2 * CH
SUB = (PATCHES[2] // PATCHES[0]) ** 2
NB = B * GRIDS[2] ** 2
FINE = GRIDS[0] ** 2
LATE = 5 * G
TOK_TILES = ([("fine", i) for i in range(LATE // 2, B // 2)] + [("mid", t) for t in range(4)] + [("large", 0)]
             + [("fine", i) for i in range(LATE // 2)])
TOK_SIZE = {"fine": 0, "mid": 1, "large": 2}
FIRST_WRITES, FINE_WRITES, COARSE_WRITES = G // 2, (B - G) // 2, 2 * 4 + 1
REST = TOK_TILES.index(("fine", 2))
FIRST_MID, LARGE = TOK_TILES.index(("mid", 0)), TOK_TILES.index(("large", 0))

KA, KB = 128, D - 128
WQ, WK, WV, WIN = 0, H * KD, 2 * H * KD, 2 * H * KD + H * VD
WCOLS = WIN + HID
WIDE_GROUPS = ((WQ, WV), (WV, WIN), (WIN, WCOLS))
RING = 4

PRE_ORDER = ([("xt", k) for k in range(KC)] + [("qk", m) for m in range(5)] + [("u", 0), ("qk", 5), ("u", 1)]
             + [("rel", r) for r in range(RBATCHES)] + [("qk", m) for m in range(6, 2 * QM)]
             + [("v", n) for n in range(2 * len(TILES))])
PRE_N = {use: n for n, use in enumerate(PRE_ORDER)}
PRE_USES = len(PRE_ORDER)
POST_WO, POST_XT, POST_UP, POST_DOWN = 0, 3, 5, 5 + MH
POST_USES = POST_DOWN + 3

LAG_SUMS, LAG_PROBS, LAG_VALUES = 1, 2, 3
GELU_SLOT = 6
PLAN = {
    (0, 0): [("v", 0), ("norm1", 0)],
    (0, 1): [("v", 1)],
    (0, 2): [("norm1", 1)],
    (1, 0): [("v", 2)],
    (1, 2): [("xt", 0)],
    (2, 0): [("qk", 0), ("qk", 1)],
    (2, 1): [("qk", 2), ("qk", 3)],
    (2, 2): [("qk", 4), ("u", 0)],
    (3, 0): [("qk", 5)],
    (3, 1): [("u", 1), ("wo", 0)],
    (4, 0): [("wo", 1)],
    (4, 1): [("rel", 0), ("rel", 1)],
    (4, 2): [("wo", 2), ("norm2", 0)],
    (5, 0): [("rel", 2), ("rel", 3), ("norm2", 1)],
    (5, 1): [("rel", 4), ("rel", 5), ("bias", 0)],
    (5, 2): [("x2t", 0)],
    (6, 0): [("qk", 6)],
    (6, 1): [("up", 0), ("up", 1)],
    (6, 2): [("up", 2), ("up", 3)],
    (7, 0): [("up", 4), ("up", 5), ("qk", 7)],
    (7, 1): [("down", 0), ("down", 1)],
    (7, 2): [("down", 2)],
}
PLAN_FIRST = {
    (0, 0): [("v", 0), ("norm1", 0)],
    (0, 1): [("v", 1)],
    (0, 2): [("norm1", 1)],
    (1, 0): [("v", 2)],
    (1, 2): [("xt", 0)],
    (2, 0): [("qk", 0), ("qk", 1)],
    (2, 1): [("qk", 2), ("qk", 3)],
    (2, 2): [("qk", 4), ("u", 0)],
    (3, 0): [("qk", 5)],
    (3, 1): [("u", 1)],
    (4, 0): [("rel", 0), ("rel", 1)],
    (5, 0): [("rel", 2), ("rel", 3), ("bias", 0)],
    (6, 0): [("rel", 4), ("rel", 5), ("qk", 6)],
    (7, 0): [("qk", 7)],
}
PLAN_LAST = {
    (0, 0): [("v", 0)],
    (0, 1): [("v", 1)],
    (1, 0): [("v", 2)],
    (2, 0): [("wo", 0)],
    (3, 0): [("wo", 1)],
    (3, 2): [("wo", 2), ("norm2", 0)],
    (4, 0): [("norm2", 1)],
    (5, 0): [("x2t", 0)],
    (6, 0): [("up", 0), ("up", 1)],
    (6, 1): [("up", 2), ("up", 3)],
    (6, 2): [("up", 4), ("up", 5)],
    (7, 0): [("down", 0)],
    (7, 1): [("down", 1)],
    (7, 2): [("down", 2)],
}
TAIL_WO = {0: 0, 2: 1}
OF_POST = ("wo", "norm2", "x2t", "up", "down")
assert PRE_N["qk", QM - 1] % 2 == PRE_N["u", 0] % 2 and T % J == 1
assert PRE_USES % 2 == 0 and POST_USES % 2 == 0


def positional_windows():
    nb = RF // 2
    rate = np.exp(np.log(T + 1) / nb).astype(np.float32)
    widths = rate ** np.arange(1, nb + 1, dtype=np.float32) - np.float32(1)
    pos = np.arange(RWIN)[None, :] - np.arange(J)[:, None] - (T - 1)
    inside = (widths[None, :, None] > np.abs(pos)[:, None, :]).astype(np.float32)
    signed = np.sign(pos)[:, None, :] * inside
    return np.concatenate([inside, signed], axis=1).reshape(J * RF, RWIN).astype(np.float32)


def build(nc, ins, out):
    with ExitStack() as ctx:
        def sb(name, shape, dtype=F32):
            return ctx.enter_context(nc.sbuf_tensor(name, shape, dtype))

        def psum(name):
            return ctx.enter_context(nc.psum_tensor(name, [128, 512], F32))

        def sem(name):
            return ctx.enter_context(nc.semaphore(name))

        b_tok = sb("b_tok", [128, 3, D])
        w_hi = sb("w_hi", [128, WCOLS], F32R)
        w_lo = sb("w_lo", [128, WCOLS], F32R)
        w_bhi = sb("w_bhi", [128, WCOLS], F32R)
        w_blo = sb("w_blo", [128, WCOLS], F32R)
        w_rkt = sb("w_rkt", [128, HH, RF])
        rw_bias = sb("rw_bias", [128, QM])
        rr_bias = sb("rr_bias", [128, QM])
        r_diff = sb("r_diff", [128, QM])
        w_o = sb("w_o", [128, OC, D])
        b_o = sb("b_o", [128, D])
        b_in = sb("b_in", [128, MH])
        w_out = sb("w_out", [128, MH, D])
        ident = sb("ident", [128, 128])
        windows = sb("windows", [J * RF, RWIN])
        u_bias = sb("u_bias", [J * RF, H])
        zeros_bf = sb("zeros_bf", [128, 128], mybir.dt.bfloat16)

        neg_half = sb("neg_half", [128, 3])
        eps = sb("eps", [128, 3])
        spare = sb("spare", [1, 2])

        arena_v = sb("arena_v", [128, 2 * G * H * VD])
        v_sb = arena_v[:, :].rearrange("p (r i h v) -> p r i h v", r=2, i=G, h=H)
        w_tok2 = arena_v[0:DK, 0:KC * SUB * D].rearrange("p (k s d) -> p k s d", k=KC, s=SUB)
        arena_r = sb("arena_r", [128, 2 * HB * T])
        rel_sb = arena_r[:, :].rearrange("p (r n t) -> p r n t", r=2, n=HB)
        pix = arena_r[0:DK, 0:KC * SUB * NB].rearrange("p (k s n) -> p k s n", k=KC, s=SUB)
        k_sb = sb("k_sb", [128, 2, QM, NT])
        arena_k = k_sb[:, :, :, :].rearrange("p r m n -> p (r m n)")
        w_tok0 = arena_k[0:DK, 0:KC * D].rearrange("p (k d) -> p k d", k=KC)
        w_tok1 = arena_k[0:DK, KC * D:5 * KC * D].rearrange("p (k s d) -> p k s d", k=KC, s=4)
        arena_p = sb("arena_p", [128, max(3 * RING * HT, len(TOK_TILES) * D)])
        tok_sb = arena_p[:, 0:len(TOK_TILES) * D].rearrange("p (r d) -> p r d", r=len(TOK_TILES))
        hid = sb("hid", [128, MH, NT])
        pix_rest = hid[0:DK, :, :].rearrange("p m n -> p (m n)")[:, 0:KC * (B - LATE) * FINE].rearrange(
            "p (k n) -> p k n", k=KC)

        v_tiles = sb("v_tiles", [128, len(TILES), H * VD])

        h_in = sb("h_in", [128, 2, 3, D])
        h_bo = sb("h_bo", [128, 2, 3, D])
        ln1_stats = sb("ln1_stats", [128, 3, 6])
        ln1_mv = sb("ln1_mv", [128, 3, 2])
        ln1_rstd = sb("ln1_rstd", [128, 3])
        xn = sb("xn", [128, 3, D])
        x_hi = sb("x_hi", [128, NT], F32R)
        x_lo = sb("x_lo", [128, NT], F32R)
        x_b = sb("x_b", [128, NT], F32R)
        q_sb = sb("q_sb", [128, 2, QM, NT])
        u_diag = sb("u_diag", [J * RF, J, H, G, RG])
        pix_late = u_diag[0:DK].rearrange("p j h i g -> p (j h i g)")[:, 0:KC * LATE * FINE].rearrange(
            "p (k n) -> p k n", k=KC)
        u_rows = sb("u_rows", [J * RF, HH, G, RG])

        st_sb = sb("st_sb", [T, 2, HH, T])
        smax = sb("smax", [T, 2, HH])
        shifted = sb("shifted", [T, 2, HH, T])
        prob, probn, pt_sb = (arena_p[0:T, i * RING * HT:(i + 1) * RING * HT].rearrange(
            "p (r h t) -> p r h t", r=RING, h=HH) for i in range(3))
        psums = sb("psums", [T, RING, HH])
        precip = sb("precip", [T, RING, HH])
        arena_o = sb("arena_o", [128, WCOLS])
        ot_sb = arena_o[:, 0:OC * NT].rearrange("p (c n) -> p c n", c=OC)
        w_a_raw = arena_o[:, 0:WCOLS]
        w_b_raw = q_sb[:, :, :, :].rearrange("p r m n -> p (r m n)")[:, 0:WCOLS]
        h1 = sb("h1", [128, 3, D])
        ln2_stats = sb("ln2_stats", [128, 3, 6])
        ln2_mv = sb("ln2_mv", [128, 3, 2])
        ln2_rstd = sb("ln2_rstd", [128, 3])
        x2 = sb("x2", [128, 3, D])
        x2_hi = sb("x2_hi", [128, NT], F32R)
        x2_lo = sb("x2_lo", [128, NT], F32R)
        x2_b = sb("x2_b", [128, NT], F32R)
        y_sb = sb("y_sb", [128, 3, D])

        s_ps = [psum("s_ps0"), psum("s_ps1")]
        pt_ps, ot_ps = psum("pt_ps"), psum("ot_ps")
        pre_ps = [psum("pre_ps0"), psum("pre_ps1")]
        post_ps = [psum("post_ps0"), psum("post_ps1")]
        tok_ps = [pre_ps[0], pre_ps[1], post_ps[0], post_ps[1], s_ps[0], ot_ps]

        h_dram = nc.dram_tensor("h_scratch", (B, T, D), F32, kind="Internal").ap()
        h_rows = h_dram.rearrange("b t d -> (b t) d")
        out_rows = out.rearrange("b t d -> (b t) d")

        ld = {n: sem("ld_" + n) for n in (
            "w0", "fine", "late", "pix", "w1", "w2", "btok", "qk", "v", "u", "rwb", "o", "in", "bin", "out", "const")}
        tok_mm = sem("tok_mm")
        tok_add = sem("tok_add")
        fine_wr = sem("fine_wr")
        coarse_wr = sem("coarse_wr")
        first_wr = sem("first_wr")
        cls_wr = sem("cls_wr")
        cleared = sem("cleared")
        w_hi_done = sem("w_hi_done")
        w_split = sem("w_split")
        diff_done = sem("diff_done")
        x_hi_done = sem("x_hi_done")
        x2_hi_done = sem("x2_hi_done")
        u_mm = sem("u_mm")
        u_placed = sem("u_placed")
        u_ready = sem("u_ready")
        h_ld = [sem("h_ld0"), sem("h_ld1")]
        hbo_done = sem("hbo_done")
        ln1_step = sem("ln1_step")
        ln2_step = sem("ln2_step")
        ln1_rstd_step = sem("ln1_rstd_step")
        ln2_rstd_step = sem("ln2_rstd_step")
        pre_full = [sem("pre_full0"), sem("pre_full1")]
        pre_evac = [sem("pre_evac0"), sem("pre_evac1")]
        post_full = [sem("post_full0"), sem("post_full1")]
        post_evac = [sem("post_evac0"), sem("post_evac1")]
        st_full = [sem("st_full0"), sem("st_full1")]
        st_evac = [sem("st_evac0"), sem("st_evac1")]
        s_full = [sem("s_full0"), sem("s_full1")]
        s_evac = [sem("s_evac0"), sem("s_evac1")]
        max_done = sem("max_done")
        exp_done = sem("exp_done")
        sum_done = sem("sum_done")
        recip_done = sem("recip_done")
        probn_done = sem("probn_done")
        pt_full, pt_evac = sem("pt_full"), sem("pt_evac")
        ot_full, ot_evac = sem("ot_full"), sem("ot_evac")
        v_moved = sem("v_moved")
        y_out = sem("y_out")

        block = ctx.enter_context(nc.Block())

        def wait(eng, s, value):
            if isinstance(value, int) and value <= 0:
                return
            eng.wait_ge(s, value)

        def pre_count(q, n):
            return q * (PRE_USES // 2) + (n // 2 + 1)

        def post_count(q, n):
            return q * (POST_USES // 2) + (n // 2 + 1)

        def lagged(q, par, slot, lag):
            if slot >= lag:
                return None if isinstance(q, int) and q == NQ else (q, par, slot - lag, q * HALVES + (slot - lag))
            if isinstance(q, int) and q == 0:
                return None
            k = slot - lag + HALVES
            return (q - 1, 1 - par, k, q * HALVES + (slot - lag))

        def image(where):
            q, _, k, _ = where
            return q * G + k // 2, k % 2

        def ring(where):
            return where[2] % RING

        def dense(work, q, par, slot, part, pre, post):
            plan = PLAN if pre and post else PLAN_FIRST if pre else PLAN_LAST
            for kind, n in plan.get((slot, part), ()):
                if kind not in work:
                    continue
                if kind == "v":
                    work[kind](q, par, n)
                elif kind in OF_POST:
                    work[kind](q - 1, 1 - par, n)
                else:
                    work[kind](q + 1, 1 - par, n)

        def rel_copies(par, r):
            bank = pre_ps[PRE_N["rel", r] % 2]
            first = r * RBATCH
            whole = min(RBATCH, T // J - first)
            pairs = [(rel_sb[0:T, par, :, J * first:J * (first + whole)].rearrange("p n (g j) -> p n g j", j=J),
                      bank[0:T, 0:whole * J * HB].rearrange("p (g j n) -> p n g j", g=whole, j=J))]
            if first + whole < min(first + RBATCH, RG):
                js = T - J * (first + whole)
                pairs.append((rel_sb[0:T, par, :, J * (first + whole):T],
                              bank[0:T, whole * J * HB:(whole * J + js) * HB].rearrange("p (j n) -> p n j", j=js)))
            return pairs

        def passes(eng, iteration, tail):
            iteration(0, 0, pre=True, post=False)
            with eng.Fori(1, NQ - 1, 2) as q:
                iteration(q, 1, pre=True, post=True)
                iteration(q + 1, 0, pre=True, post=True)
            iteration(NQ - 1, 1, pre=False, post=True)
            tail(NQ, 0)

        @block.sync
        def _(sp):
            def load_weights(name, c0, c1):
                sp.dma_start(w_a_raw[:, c0:c1], ins["w_a"][:, c0:c1]).then_inc(ld[name], 16)
                sp.dma_start(w_b_raw[:, c0:c1], ins["w_b"][:, c0:c1]).then_inc(ld[name], 16)

            sp.dma_start(w_tok0, ins["w0"]).then_inc(ld["w0"], 16)
            sp.dma_start(pix_rest, ins["pix_fine"][:, :, LATE * FINE:]).then_inc(ld["fine"], 16)
            sp.dma_start(b_tok[:, :, :], ins["b_tok"]).then_inc(ld["btok"], 16)
            sp.dma_start(w_tok1, ins["w1"]).then_inc(ld["w1"], 16)
            for k in range(KC):
                sp.dma_start(pix[:, k], ins["pix"][:, k]).then_inc(ld["pix"], 16)
            sp.dma_start(pix_late, ins["pix_fine"][:, :, 0:LATE * FINE]).then_inc(ld["late"], 16)
            for k in range(KC):
                sp.dma_start(w_tok2[:, k], ins["w2"][:, k]).then_inc(ld["w2"], 16)
            sp.dma_start(w_rkt[:, :, :], ins["w_rkt"]).then_inc(ld["u"], 16)
            sp.dma_start(rr_bias[:, :], ins["rr_bias"]).then_inc(ld["u"], 16)
            sp.dma_start(rw_bias[:, :], ins["rw_bias"]).then_inc(ld["rwb"], 16)
            sp.dma_start(ident[:, :], ins["ident"]).then_inc(ld["const"], 16)
            sp.dma_start(windows[:, :], ins["windows"]).then_inc(ld["const"], 16)
            sp.dma_start(b_o[:, :], ins["b_o"]).then_inc(ld["const"], 16)
            load_weights("qk", WQ, WV)
            load_weights("v", WV, WIN)
            sp.dma_start(w_o[:, :, :], ins["w_o"]).then_inc(ld["o"], 16)
            load_weights("in", WIN, WCOLS)
            sp.dma_start(b_in[:, :], ins["b_in"]).then_inc(ld["bin"], 16)
            sp.dma_start(w_out[:, :, :], ins["w_out"]).then_inc(ld["out"], 16)

            def load_quad(q, par):
                wait(sp, ln1_step, (q - 1) * 9)
                wait(sp, hbo_done, q - 1)
                for j, (t0, rows) in enumerate(TILES):
                    sp.dma_start(h_in[0:rows, par, j, :],
                                 h_rows[bass.ds(q * NT + t0, rows), :]).then_inc(h_ld[par], 16)

            def move_values(q, par):
                wait(sp, ot_full, (q - 1) * HALVES + 1)
                for move, (j, rows, img, tokens) in enumerate(V_MOVES):
                    if move == 0 or V_MOVES[move - 1][0] < j:
                        for half in range(2):
                            n = PRE_N["v", 2 * j + half]
                            sp.wait_ge(pre_evac[n % 2], pre_count(q, n))
                    sp.dma_start(v_sb[tokens, par, img].rearrange("p h v -> p (h v)"),
                                 v_tiles[rows, j, :]).then_inc(v_moved, 16)

            def store_quad(q):
                for j, (t0, rows) in enumerate(TILES):
                    sp.wait_ge(post_evac[(POST_DOWN + j) % 2], post_count(q, POST_DOWN + j))
                    sp.dma_start(out_rows[bass.ds(q * NT + t0, rows), :],
                                 y_sb[0:rows, j, :]).then_inc(y_out, 16)

            sp.wait_ge(coarse_wr, COARSE_WRITES * 16)
            sp.wait_ge(first_wr, FIRST_WRITES * 16)
            sp.wait_ge(cls_wr, 16)
            sp.wait_ge(cleared, 1)
            load_quad(0, 0)
            for i in range(REST, len(TOK_TILES)):
                t = TOK_TILES[i][1]
                sp.wait_ge(tok_add, i + 1)
                sp.dma_start(h_dram[2 * t:2 * t + 2, FIRST_TOKEN[0]:FIRST_TOKEN[1], :],
                             tok_sb[:, i, :]).then_inc(fine_wr, 16)
            sp.wait_ge(fine_wr, FINE_WRITES * 16)
            load_quad(1, 1)
            move_values(0, 0)
            load_quad(2, 0)
            with sp.Fori(1, NQ - 3, 1 + 1) as q:
                move_values(q, 1)
                load_quad(q + 2, 1)
                store_quad(q - 1)
                move_values(q + 1, 0)
                load_quad(q + 3, 0)
                store_quad(q)
            for q in range(NQ - 3, NQ + 1):
                if q < NQ:
                    move_values(q, q % 2)
                if q + 2 < NQ:
                    load_quad(q + 2, (q + 2) % 2)
                store_quad(q - 1)
            sp.wait_ge(y_out, NQ * 3 * 16 + 16)

        @block.gpsimd
        def _(pool):
            pool.dma_start(h_dram[:, 0, :], ins["cls"]).then_inc(cls_wr, 16)
            nc.gpsimd.memset(neg_half[:, :], -0.5)
            nc.gpsimd.memset(eps[:, :], EPS).then_inc(y_out, 16)
            for buf in (h_in, h_bo, ln1_mv, ln2_mv):
                nc.gpsimd.memset(buf[tuple(slice(None) for _ in buf.shape)], 0.0)
            nc.gpsimd.memset(h1[:, :, :], 0.0).then_inc(cleared, 1)
            nc.gpsimd.memset(zeros_bf[:, :], 0.0).then_inc(cleared, 1)

            def split(group):
                c0, c1 = WIDE_GROUPS[group]
                for part, (raw, hi, lo) in enumerate(((w_a_raw, w_hi, w_lo), (w_b_raw, w_bhi, w_blo))):
                    pool.wait_ge(w_hi_done, 2 * group + part + 1)
                    nc.gpsimd.tensor_tensor(lo[:, c0:c1], raw[:, c0:c1], hi[:, c0:c1].bitcast(F32),
                                            ALU.subtract).then_inc(w_split, 1)

            def bias(q, par, _):
                pool.wait_ge(h_ld[par], (q - par) * 24 + 48)
                wait(pool, post_evac[0], post_count(q - 2, POST_WO + 2))
                wait(pool, post_evac[1], post_count(q - 2, POST_WO + 1))
                nc.gpsimd.tensor_tensor(h_bo[:, par], h_in[:, par],
                                        b_o[:, :].unsqueeze(1).to_broadcast([128, 3, D]),
                                        ALU.add).then_inc(hbo_done, 1)

            def rstd(q, step, rstd_step, mv, out):
                pool.wait_ge(step, q * 9 + 6)
                nc.gpsimd.tensor_tensor(out[:, :], mv[:, :, 1], eps[:, :], ALU.add).then_inc(rstd_step, 1)
                pool.wait_ge(rstd_step, 2 * q + 1)
                nc.gpsimd.tensor_tensor(out[:, :], out[:, :], neg_half[:, :], ALU.pow).then_inc(rstd_step, 1)

            def normalize(where):
                if where is None:
                    return
                a, buf = where[3], ring(where)
                pool.wait_ge(recip_done, a + 1)
                wait(pool, pt_full, a - RING + 1)
                nc.gpsimd.tensor_tensor(probn[:, buf], prob[:, buf],
                                        precip[:, buf].unsqueeze(2).to_broadcast([T, HH, T]),
                                        ALU.mult).then_inc(probn_done, 1)

            work = {
                "norm1": lambda q, par, part: part or rstd(q, ln1_step, ln1_rstd_step, ln1_mv, ln1_rstd),
                "norm2": lambda q, par, part: part or rstd(q, ln2_step, ln2_rstd_step, ln2_mv, ln2_rstd),
                "bias": bias,
            }

            def iteration(q, par, pre, post):
                for slot in range(HALVES):
                    dense(work, q, par, slot, 0, pre, post)
                    dense(work, q, par, slot, 1, pre, post)
                    normalize(lagged(q, par, slot, LAG_SUMS))
                    dense(work, q, par, slot, 2, pre, post)

            def tail(q, par):
                for slot in range(LAG_SUMS):
                    normalize(lagged(q, par, slot, LAG_SUMS))
                work["norm2"](q - 1, 1 - par, 0)

            split(0)
            split(1)
            work["norm1"](0, 0, 0)
            pool.wait_ge(tok_mm, len(TOK_TILES))
            nc.gpsimd.memset(u_diag[:, :, :, :, :], 0.0).then_inc(cleared, 1)
            pool.wait_ge(ld["const"], 48)
            bias(0, 0, 0)
            split(2)
            passes(pool, iteration, tail)

        @block.tensor
        def _(pe):
            def bias_products():
                pe.wait_ge(ld["u"], 32)
                pe.wait_ge(diff_done, 1)
                for j in range(J):
                    for h in range(H):
                        p = KD * (h % 2)
                        bank = (s_ps[1], pt_ps)[h % 2]
                        last = nc.tensor.matmul(bank[j * RF:(j + 1) * RF, h // 2:h // 2 + 1],
                                                w_rkt[p:p + KD, h // 2, :], r_diff[p:p + KD, h // 2:h // 2 + 1],
                                                start=True, stop=True)
                last.then_inc(u_mm, 1)

            for i, (kind, t) in enumerate(TOK_TILES):
                if i == 0:
                    pe.wait_ge(ld["w0"], 16)
                    pe.wait_ge(ld["fine"], 16)
                if i == FIRST_MID:
                    pe.wait_ge(ld["w1"], 16)
                    pe.wait_ge(ld["pix"], 32)
                if i == LARGE:
                    bias_products()
                    pe.wait_ge(ld["w2"], 32)
                if kind == "fine":
                    if i == LARGE + 1:
                        pe.wait_ge(ld["late"], 16)
                    source, c = (pix_late, 2 * t * FINE) if 2 * t < LATE else (pix_rest, (2 * t - LATE) * FINE)
                    products = [(source[:, k, c:c + 128], w_tok0[:, k, :]) for k in range(KC)]
                elif kind == "mid":
                    yb, xb = divmod(t, 2)
                    products = [(pix[:, k, (2 * yb + ya) * 4 + 2 * xb + xa, :], w_tok1[:, k, 2 * ya + xa, :])
                                for ya in range(2) for xa in range(2) for k in range(KC)]
                else:
                    products = [(pix[:, k, s, :], w_tok2[:, k, s, :]) for k in range(KC) for s in range(SUB)]
                wait(pe, tok_add, i - len(tok_ps) + 1)
                for n, (lhs, rhs) in enumerate(products):
                    last = nc.tensor.matmul(tok_ps[i % len(tok_ps)][:, 0:D], lhs, rhs, start=(n == 0),
                                            stop=(n == len(products) - 1))
                last.then_inc(tok_mm, 1)

            def pre_use(q, n):
                wait(pe, pre_evac[n % 2], q * (PRE_USES // 2) + n // 2)
                return pre_ps[n % 2]

            def xt(q, par, _):
                pe.wait_ge(ln1_step, (q + 1) * 9)
                banks = [pre_use(q, PRE_N["xt", k]) for k in range(KC)]
                for k, (row, rows) in enumerate(((0, KA), (KA, KB))):
                    bank = banks[k]
                    for j, (t0, tokens) in enumerate(TILES):
                        last = nc.tensor.transpose(bank[0:rows, t0:t0 + tokens], xn[0:tokens, j, row:row + rows],
                                                   ident[0:tokens, 0:tokens])
                    last.then_inc(pre_full[PRE_N["xt", k] % 2], 1)

            def qk(q, par, m):
                n = PRE_N["qk", m]
                c = WQ + m * 128
                bank = pre_use(q, n)
                passes_of = [(w_hi, x_hi), (w_hi, x_lo), (w_lo, x_hi), (w_bhi, x_b), (w_blo, x_b)]
                for i, (w, x) in enumerate(passes_of):
                    if m == 0 and i in (0, 3):
                        k = i // 3
                        pe.wait_ge(pre_evac[PRE_N["xt", k] % 2], pre_count(q, PRE_N["xt", k]))
                    last = nc.tensor.matmul(bank[:, 0:NT], w[:, c:c + 128], x[:, :], start=(i == 0),
                                            stop=(i == len(passes_of) - 1))
                last.then_inc(pre_full[n % 2], 1)

            def v(q, par, j):
                t0, rows = TILES[j]
                tok = slice(t0, t0 + rows)
                passes_of = [(x_hi, w_hi), (x_hi, w_lo), (x_lo, w_hi), (x_b, w_bhi), (x_b, w_blo)]
                for half in range(2):
                    n = PRE_N["v", 2 * j + half]
                    bank = pre_use(q, n)
                    c = WV + half * HH * VD
                    for i, (x, w) in enumerate(passes_of):
                        last = nc.tensor.matmul(bank[0:rows, 0:HH * VD], x[:, tok], w[:, c:c + HH * VD],
                                                start=(i == 0), stop=(i == len(passes_of) - 1))
                    last.then_inc(pre_full[n % 2], 1)

            def u(q, par, half):
                n = PRE_N["u", half]
                bank = pre_use(q, n)
                m = QM - 2
                pe.wait_ge(pre_evac[PRE_N["qk", m] % 2], pre_count(q, PRE_N["qk", m]))
                nc.tensor.ldweights(zeros_bf[:, :], tile_position=(0, 0))
                p = KD * half
                for hh in range(HH):
                    for j in range(J):
                        count = len(range(j, T, J))
                        o = bank[j * RF:(j + 1) * RF, hh * G * RG:(hh + 1) * G * RG]
                        o = o.rearrange("p (i g) -> p i g", i=G)[:, :, 0:count]
                        qj = q_sb[p:p + KD, par, hh, :].rearrange("p (i t) -> p i t", i=G)[:, :, j::J]
                        last = nc.tensor.matmul(o, w_rkt[p:p + KD, hh, :], qj, start=True, stop=True)
                last.then_inc(pre_full[n % 2], 1)

            def rel(q, par, r):
                n = PRE_N["rel", r]
                bank = pre_use(q, n)
                if r == 0:
                    pe.wait_ge(u_placed, 2 * (q + 1))
                for g in range(r * RBATCH, min((r + 1) * RBATCH, RG)):
                    js = min(J, T - g * J)
                    c = (g - r * RBATCH) * J * HB
                    last = nc.tensor.matmul(bank[0:T, c:c + js * HB], windows[:, T - 1 - J * g:2 * T - 1 - J * g],
                                            u_diag[:, 0:js, :, :, g].rearrange("p j h i -> p j (h i)"),
                                            start=True, stop=True)
                last.then_inc(pre_full[n % 2], 1)

            def content(where):
                if where is None or where[2] % 2:
                    return
                q, par, k, _ = where
                img, n = k // 2, image(where)[0]
                if k == 0:
                    for m in (2 * QM - 2, 2 * QM - 1):
                        pe.wait_ge(pre_evac[PRE_N["qk", m] % 2], pre_count(q, PRE_N["qk", m]))
                for half in range(2):
                    wait(pe, s_evac[half], n)
                tok = slice(img * T, (img + 1) * T)
                for hh in range(HH):
                    for half in range(2):
                        p = KD * half
                        last = nc.tensor.matmul(s_ps[half][0:T, hh * T:(hh + 1) * T], k_sb[p:p + KD, par, hh, tok],
                                                q_sb[p:p + KD, par, hh, tok], start=True, stop=True)
                        if hh == HH - 1:
                            last.then_inc(st_full[half], 1)

            def scores_transpose(where):
                if where is None:
                    return
                n, half = image(where)
                pe.wait_ge(st_evac[half], n + 1)
                for hh in range(HH):
                    last = nc.tensor.transpose(s_ps[half][0:T, hh * T:(hh + 1) * T], st_sb[:, half, hh, :],
                                               ident[0:T, 0:T])
                last.then_inc(s_full[half], 1)

            def probs_transpose(where):
                if where is None:
                    return
                a, buf = where[3], ring(where)
                pe.wait_ge(probn_done, a + 1)
                wait(pe, pt_evac, a)
                for hh in range(HH):
                    last = nc.tensor.transpose(pt_ps[0:T, hh * T:(hh + 1) * T], probn[:, buf, hh, :], ident[0:T, 0:T])
                last.then_inc(pt_full, 1)

            def weighted_values(where):
                if where is None:
                    return
                q, par, k, a = where
                img, half = divmod(k, 2)
                if k == 0:
                    pe.wait_ge(v_moved, (q + 1) * 16 * len(V_MOVES))
                pe.wait_ge(pt_evac, a + 1)
                wait(pe, ot_evac, a)
                for piece in range(OQ):
                    hh, v0 = divmod(piece * 32, VD)
                    row, c = 32 * (piece % 4), piece // 4
                    last = nc.tensor.matmul(ot_ps[row:row + 32, c * T:(c + 1) * T],
                                            v_sb[0:T, par, img, 2 * hh + half, v0:v0 + 32],
                                            pt_sb[:, ring(where), hh, :], start=True, stop=True)
                last.then_inc(ot_full, 1)

            def post_use(q, n):
                if n >= 2:
                    wait(pe, post_evac[n % 2], q * (POST_USES // 2) + n // 2)
                return post_ps[n % 2]

            def wo(q, par, j):
                t0, rows = TILES[j]
                n = POST_WO + j
                bank = post_use(q, n)
                halves = 2 * (-(-(t0 + rows) // T))
                pe.wait_ge(ot_evac, q * HALVES + halves)
                for c in range(OC):
                    last = nc.tensor.matmul(bank[0:rows, 0:D], ot_sb[:, c, t0:t0 + rows], w_o[:, c, :],
                                            start=(c == 0), stop=(c == OC - 1))
                last.then_inc(post_full[n % 2], 1)

            def x2t(q, par, _):
                pe.wait_ge(ln2_step, (q + 1) * 9)
                banks = [post_use(q, POST_XT + k) for k in range(KC)]
                for k, (row, rows) in enumerate(((0, KA), (KA, KB))):
                    n = POST_XT + k
                    bank = banks[k]
                    for j, (t0, tokens) in enumerate(TILES):
                        last = nc.tensor.transpose(bank[0:rows, t0:t0 + tokens], x2[0:tokens, j, row:row + rows],
                                                   ident[0:tokens, 0:tokens])
                    last.then_inc(post_full[n % 2], 1)

            def up(q, par, m):
                n = POST_UP + m
                c = WIN + m * 128
                bank = post_use(q, n)
                if m == 0:
                    pe.wait_ge(w_split, 6)
                passes_of = [(w_hi, x2_hi), (w_hi, x2_lo), (w_lo, x2_hi), (w_bhi, x2_b), (w_blo, x2_b)]
                for i, (w, x) in enumerate(passes_of):
                    if m == 0 and i in (0, 3):
                        k = i // 3
                        pe.wait_ge(post_evac[(POST_XT + k) % 2], post_count(q, POST_XT + k))
                    last = nc.tensor.matmul(bank[:, 0:NT], w[:, c:c + 128], x[:, :], start=(i == 0),
                                            stop=(i == len(passes_of) - 1))
                last.then_inc(post_full[n % 2], 1)

            def down(q, par, j):
                t0, rows = TILES[j]
                n = POST_DOWN + j
                bank = post_use(q, n)
                if j == 0:
                    for m in (MH - 2, MH - 1):
                        pe.wait_ge(post_evac[(POST_UP + m) % 2], post_count(q, POST_UP + m))
                for m in range(MH):
                    last = nc.tensor.matmul(bank[0:rows, 0:D], hid[:, m, t0:t0 + rows], w_out[:, m, :],
                                            start=(m == 0), stop=(m == MH - 1))
                last.then_inc(post_full[n % 2], 1)

            work = {"xt": xt, "qk": qk, "v": v, "u": u, "rel": rel, "wo": wo, "x2t": x2t, "up": up, "down": down}

            def iteration(q, par, pre, post):
                for slot in range(HALVES):
                    content(lagged(q, par, slot, 0))
                    dense(work, q, par, slot, 0, pre, post)
                    scores_transpose(lagged(q, par, slot, 0))
                    dense(work, q, par, slot, 1, pre, post)
                    probs_transpose(lagged(q, par, slot, LAG_PROBS))
                    dense(work, q, par, slot, 2, pre, post)
                    weighted_values(lagged(q, par, slot, LAG_VALUES))

            def tail(q, par):
                for slot in range(LAG_VALUES):
                    if slot < LAG_PROBS:
                        probs_transpose(lagged(q, par, slot, LAG_PROBS))
                    if slot in TAIL_WO:
                        wo(q - 1, 1 - par, TAIL_WO[slot])
                    weighted_values(lagged(q, par, slot, LAG_VALUES))
                wo(q - 1, 1 - par, 2)
                x2t(q - 1, 1 - par, 0)
                for m in range(MH):
                    up(q - 1, 1 - par, m)
                for j in range(3):
                    down(q - 1, 1 - par, j)

            pe.wait_ge(ld["const"], 48)
            pe.wait_ge(cleared, 2)
            xt(0, 0, 0)
            pe.wait_ge(w_split, 2)
            pe.wait_ge(u_ready, 1)
            for kind, n in PRE_ORDER[KC:]:
                if kind != "v":
                    work[kind](0, 0, n)
            pe.wait_ge(w_split, 4)
            for name, count in (("o", 16), ("out", 16)):
                pe.wait_ge(ld[name], count)
            passes(pe, iteration, tail)

        @block.scalar
        def _(act):
            def xt(q, par, _):
                for k, (rows, dst) in enumerate(((KA, x_hi), (KB, x_b))):
                    n = PRE_N["xt", k]
                    act.wait_ge(pre_full[n % 2], pre_count(q, n))
                    nc.scalar.copy(dst[0:rows, :], pre_ps[n % 2][0:rows, 0:NT]).then_inc(x_hi_done, 1)

            def qk(q, par, m):
                if m >= QM:
                    return
                n = PRE_N["qk", m]
                act.wait_ge(pre_full[n % 2], pre_count(q, n))
                nc.scalar.activation(q_sb[:, par, m, :], pre_ps[n % 2][:, 0:NT], ACT.Identity,
                                     bias=rw_bias[:, m:m + 1], scale=QSCALE).then_inc(pre_evac[n % 2], 1)

            def v(q, par, j):
                rows = TILES[j][1]
                if j == 0:
                    wait(act, v_moved, q * 16 * len(V_MOVES))
                for half in range(2):
                    n = PRE_N["v", 2 * j + half]
                    act.wait_ge(pre_full[n % 2], pre_count(q, n))
                    nc.scalar.copy(v_tiles[0:rows, j, half * HH * VD:(half + 1) * HH * VD],
                                   pre_ps[n % 2][0:rows, 0:HH * VD]).then_inc(pre_evac[n % 2], 1)

            def rel(q, par, r):
                if r % 2:
                    return
                n = PRE_N["rel", r]
                act.wait_ge(pre_full[n % 2], pre_count(q, n))
                for o, i in rel_copies(par, r):
                    last = nc.scalar.copy(o, i)
                last.then_inc(pre_evac[n % 2], 1)

            def exponentials(where):
                if where is None:
                    return
                a, (n, half) = where[3], image(where)
                act.wait_ge(s_evac[half], n + 1)
                wait(act, probn_done, a - RING + 1)
                nc.scalar.activation(prob[:, ring(where)], shifted[:, half],
                                     ACT.Exp).then_inc(exp_done, 1)

            def probs_copy(where):
                if where is None:
                    return
                a, buf = where[3], ring(where)
                act.wait_ge(pt_full, a + 1)
                wait(act, ot_full, a - RING + 1)
                nc.scalar.copy(pt_sb[:, buf], pt_ps[0:T, 0:HT]).then_inc(pt_evac, 1)

            def outputs_copy(where):
                if where is None:
                    return
                _, _, k, a = where
                img, half = divmod(k, 2)
                act.wait_ge(ot_full, a + 1)
                c = OC // 2
                nc.scalar.copy(ot_sb[:, half * c:(half + 1) * c, img * T:(img + 1) * T],
                               ot_ps[:, 0:c * T].rearrange("p (c t) -> p c t", c=c)).then_inc(ot_evac, 1)

            def x2t(q, par, _):
                for k, (rows, dst) in enumerate(((KA, x2_hi), (KB, x2_b))):
                    n = POST_XT + k
                    act.wait_ge(post_full[n % 2], post_count(q, n))
                    nc.scalar.copy(dst[0:rows, :], post_ps[n % 2][0:rows, 0:NT]).then_inc(x2_hi_done, 1)

            def up(q, par, m):
                n = POST_UP + m
                act.wait_ge(post_full[n % 2], post_count(q, n))
                nc.scalar.activation(hid[:, m, :], post_ps[n % 2][:, 0:NT], ACT.Gelu,
                                     bias=b_in[:, m:m + 1]).then_inc(post_evac[n % 2], 1)

            work = {"xt": xt, "qk": qk, "v": v, "rel": rel, "x2t": x2t, "up": up}

            def iteration(q, par, pre, post):
                for slot in range(HALVES):
                    dense(work, q, par, slot, 0, pre, post)
                    dense(work, q, par, slot, 1, pre, post)
                    if slot == GELU_SLOT + 1:
                        exponentials(lagged(q, par, slot - 1, 0))
                    probs_copy(lagged(q, par, slot, LAG_PROBS))
                    dense(work, q, par, slot, 2, pre, post)
                    if slot != GELU_SLOT:
                        exponentials(lagged(q, par, slot, 0))
                    outputs_copy(lagged(q, par, slot, LAG_VALUES))

            def tail(q, par):
                for slot in range(LAG_VALUES):
                    if slot < LAG_PROBS:
                        probs_copy(lagged(q, par, slot, LAG_PROBS))
                    outputs_copy(lagged(q, par, slot, LAG_VALUES))
                x2t(q - 1, 1 - par, 0)
                for m in range(MH):
                    up(q - 1, 1 - par, m)

            for i, (kind, t) in enumerate(TOK_TILES):
                if i == LARGE:
                    for name, (c0, c1) in zip(("qk", "v", "in"), WIDE_GROUPS):
                        act.wait_ge(ld[name], 32)
                        nc.scalar.copy(w_hi[:, c0:c1], w_a_raw[:, c0:c1]).then_inc(w_hi_done, 1)
                        nc.scalar.copy(w_bhi[:, c0:c1], w_b_raw[:, c0:c1]).then_inc(w_hi_done, 1)
                if i == REST:
                    break
                act.wait_ge(tok_add, i + 1)
                size = TOK_SIZE[kind]
                rows = h_dram[:, FIRST_TOKEN[size]:FIRST_TOKEN[size] + GRIDS[size] ** 2, :]
                if kind == "fine":
                    act.dma_start(rows[2 * t:2 * t + 2], tok_sb[:, i, :]).then_inc(
                        first_wr if 2 * t < G else fine_wr, 16)
                elif kind == "mid":
                    rows = rows.rearrange("b (Y y X x) d -> y x Y X b d", Y=2, X=2, y=2)[t // 2, t % 2]
                    for Y in range(2):
                        act.dma_start(rows[Y], tok_sb[64 * Y:64 * Y + 64, i, :]).then_inc(coarse_wr, 16)
                else:
                    act.dma_start(rows.rearrange("b n d -> n b d"), tok_sb[:, i, :]).then_inc(coarse_wr, 16)

            xt(0, 0, 0)
            act.wait_ge(ld["rwb"], 16)
            for kind, n in PRE_ORDER[KC:]:
                if kind in ("qk", "rel"):
                    work[kind](0, 0, n)
            act.wait_ge(ld["bin"], 16)
            act.wait_ge(coarse_wr, COARSE_WRITES * 16)
            act.wait_ge(first_wr, FIRST_WRITES * 16)
            act.wait_ge(fine_wr, FINE_WRITES * 16)
            passes(act, iteration, tail)

        @block.vector
        def _(dve):
            dve.wait_ge(ld["btok"], 16)

            def add_bias(i):
                dve.wait_ge(tok_mm, i + 1)
                kind = TOK_TILES[i][0]
                nc.vector.tensor_tensor(tok_sb[:, i, :], tok_ps[i % len(tok_ps)][:, 0:D],
                                        b_tok[:, TOK_SIZE[kind], :], ALU.add).then_inc(tok_add, 1)

            def aggregate(q, step, stats, mv):
                dve.wait_ge(step, q * 9 + 3)
                nc.vector.memset(spare[:, :], 0.0)
                for j, (_, rows) in enumerate(TILES):
                    nc.vector.bn_aggr(mv[0:rows, j, :], stats[0:rows, j, :]).then_inc(step, 1)

            def normalize(q, step, rstd_step, src, mv, rstd, dst):
                dve.wait_ge(rstd_step, 2 * (q + 1))
                for j, (_, rows) in enumerate(TILES):
                    nc.vector.tensor_scalar(dst[0:rows, j, :], src[0:rows, j, :], mv[0:rows, j, 0:1],
                                            rstd[0:rows, j:j + 1], ALU.subtract, ALU.mult).then_inc(step, 1)

            def norm1(q, par, part):
                if part == 0:
                    dve.wait_ge(h_ld[par], (q - par) * 24 + 48)
                    for j, (_, rows) in enumerate(TILES):
                        nc.vector.bn_stats(ln1_stats[0:rows, j, :], h_in[0:rows, par, j, :]).then_inc(ln1_step, 1)
                    aggregate(q, ln1_step, ln1_stats, ln1_mv)
                else:
                    normalize(q, ln1_step, ln1_rstd_step, h_in[:, par], ln1_mv, ln1_rstd, xn)

            def xt(q, par, _):
                for k, (src, dst) in enumerate(((x_hi, x_lo[:, :]), (x_b, x_b[KB:2 * KB, :]))):
                    n = PRE_N["xt", k]
                    rows = (KA, KB)[k]
                    dve.wait_ge(x_hi_done, 2 * q + (k + 1))
                    nc.vector.tensor_tensor(dst, pre_ps[n % 2][0:rows, 0:NT], src[0:rows, :].bitcast(F32),
                                            ALU.subtract).then_inc(pre_evac[n % 2], 1)

            def qk(q, par, m):
                if m < QM:
                    return
                n = PRE_N["qk", m]
                dve.wait_ge(pre_full[n % 2], pre_count(q, n))
                nc.vector.tensor_copy(k_sb[:, par, m - QM, :], pre_ps[n % 2][:, 0:NT]).then_inc(pre_evac[n % 2], 1)

            def u(q, par, half):
                n = PRE_N["u", half]
                dve.wait_ge(pre_full[n % 2], pre_count(q, n))
                wait(dve, u_placed, 2 * q + half)
                heads = slice(half, H, 2)
                ps = pre_ps[n % 2][:, 0:HH * G * RG].rearrange("p (h i g) -> p h i g", h=HH, i=G)
                for rows, g0, g1 in ((slice(0, J * RF), 0, T // J), (slice(0, RF), T // J, RG)):
                    by_head = u_bias[rows, heads].unsqueeze(2).unsqueeze(3).to_broadcast(
                        [rows.stop, HH, G, g1 - g0])
                    last = nc.vector.tensor_tensor(u_rows[rows, :, :, g0:g1], ps[rows, :, :, g0:g1], by_head, ALU.add)
                last.then_inc(pre_evac[n % 2], 1)
                dve.wait_ge(pre_evac[n % 2], pre_count(q, n))
                for j in range(J):
                    count = len(range(j, T, J))
                    rows = slice(j * RF, (j + 1) * RF)
                    last = nc.vector.tensor_copy(u_diag[rows, j, heads, :, 0:count], u_rows[rows, :, :, 0:count])
                last.then_inc(u_placed, 1)

            def rel(q, par, r):
                if r % 2 == 0:
                    return
                n = PRE_N["rel", r]
                dve.wait_ge(pre_full[n % 2], pre_count(q, n))
                for o, i in rel_copies(par, r):
                    last = nc.vector.tensor_copy(o, i)
                last.then_inc(pre_evac[n % 2], 1)

            def scores_add(where):
                if where is None or where[2] % 2:
                    return
                q, par, k, _ = where
                img, n = k // 2, image(where)[0]
                if k == 0:
                    for r in (RBATCHES - 2, RBATCHES - 1):
                        dve.wait_ge(pre_evac[PRE_N["rel", r] % 2], pre_count(q, PRE_N["rel", r]))
                for half in range(2):
                    dve.wait_ge(st_full[half], n + 1)
                    rel = rel_sb[0:T, par].rearrange("p (h i) t -> p h i t", i=G)[:, half::2, img, :]
                    nc.vector.tensor_tensor(st_sb[:, half], s_ps[half][0:T, 0:HT].rearrange("p (h t) -> p h t", h=HH),
                                            rel, ALU.add).then_inc(st_evac[half], 1)

            def scores_shift(where):
                if where is None:
                    return
                a, (n, half) = where[3], image(where)
                ps = s_ps[half][0:T, 0:HT].rearrange("p (h t) -> p h t", h=HH)
                dve.wait_ge(s_full[half], n + 1)
                nc.vector.reduce_max(smax[:, half], ps, AX.X).then_inc(max_done, 1)
                dve.wait_ge(max_done, a + 1)
                nc.vector.tensor_tensor(shifted[:, half], ps, smax[:, half].unsqueeze(2).to_broadcast([T, HH, T]),
                                        ALU.subtract).then_inc(s_evac[half], 1)

            def prob_sums(where):
                if where is None:
                    return
                a, buf = where[3], ring(where)
                dve.wait_ge(exp_done, a + 1)
                nc.vector.reduce_sum(psums[:, buf], prob[:, buf], AX.X).then_inc(sum_done, 1)
                dve.wait_ge(sum_done, a + 1)
                nc.vector.reciprocal(precip[:, buf], psums[:, buf]).then_inc(recip_done, 1)

            def wo(q, par, j):
                rows = TILES[j][1]
                n = POST_WO + j
                if j == 0:
                    dve.wait_ge(hbo_done, q + 1)
                dve.wait_ge(post_full[n % 2], post_count(q, n))
                nc.vector.tensor_tensor(h1[0:rows, j, :], post_ps[n % 2][0:rows, 0:D], h_bo[0:rows, par, j, :],
                                        ALU.add).then_inc(post_evac[n % 2], 1)
                dve.wait_ge(post_evac[n % 2], post_count(q, n))
                nc.vector.bn_stats(ln2_stats[0:rows, j, :], h1[0:rows, j, :]).then_inc(ln2_step, 1)

            def norm2(q, par, part):
                if part == 0:
                    aggregate(q, ln2_step, ln2_stats, ln2_mv)
                else:
                    normalize(q, ln2_step, ln2_rstd_step, h1, ln2_mv, ln2_rstd, x2)

            def x2t(q, par, _):
                for k, (src, dst) in enumerate(((x2_hi, x2_lo[:, :]), (x2_b, x2_b[KB:2 * KB, :]))):
                    n = POST_XT + k
                    rows = (KA, KB)[k]
                    dve.wait_ge(x2_hi_done, 2 * q + (k + 1))
                    nc.vector.tensor_tensor(dst, post_ps[n % 2][0:rows, 0:NT], src[0:rows, :].bitcast(F32),
                                            ALU.subtract).then_inc(post_evac[n % 2], 1)

            def down(q, par, j):
                rows = TILES[j][1]
                n = POST_DOWN + j
                if j == 0:
                    dve.wait_ge(y_out, q * 48 + 16)
                dve.wait_ge(post_full[n % 2], post_count(q, n))
                nc.vector.tensor_tensor(y_sb[0:rows, j, :], post_ps[n % 2][0:rows, 0:D], h1[0:rows, j, :],
                                        ALU.add).then_inc(post_evac[n % 2], 1)

            work = {"norm1": norm1, "xt": xt, "qk": qk, "u": u, "rel": rel, "wo": wo, "norm2": norm2,
                    "x2t": x2t, "down": down}

            def iteration(q, par, pre, post):
                for slot in range(HALVES):
                    scores_add(lagged(q, par, slot, 0))
                    dense(work, q, par, slot, 0, pre, post)
                    scores_shift(lagged(q, par, slot, 0))
                    dense(work, q, par, slot, 1, pre, post)
                    prob_sums(lagged(q, par, slot, LAG_SUMS))
                    dense(work, q, par, slot, 2, pre, post)

            def tail(q, par):
                for slot in range(LAG_SUMS):
                    prob_sums(lagged(q, par, slot, LAG_SUMS))
                for j in range(3):
                    wo(q - 1, 1 - par, j)
                norm2(q - 1, 1 - par, 0)
                norm2(q - 1, 1 - par, 1)
                x2t(q - 1, 1 - par, 0)
                for j in range(3):
                    down(q - 1, 1 - par, j)

            for i in range(len(TOK_TILES)):
                if i == FIRST_MID:
                    dve.wait_ge(ld["u"], 32)
                    dve.wait_ge(ld["rwb"], 16)
                    nc.vector.tensor_tensor(r_diff[:, :], rr_bias[:, :], rw_bias[:, :],
                                            ALU.subtract).then_inc(diff_done, 1)
                if i == LARGE + 1:
                    dve.wait_ge(u_mm, 1)
                    for half, bank in enumerate((s_ps[1], pt_ps)):
                        last = nc.vector.tensor_copy(u_bias[:, half::2], bank[:, 0:HH])
                    last.then_inc(u_ready, 1)
                add_bias(i)
            dve.wait_ge(cleared, 1)
            norm1(0, 0, 0)
            norm1(0, 0, 1)
            xt(0, 0, 0)
            dve.wait_ge(cleared, 3)
            for kind, n in PRE_ORDER[KC:]:
                if kind != "v":
                    work[kind](0, 0, n)
            passes(dve, iteration, tail)


def kernel(x, cls_tok, L0_tok_W0, L0_tok_b0, L0_tok_W1, L0_tok_b1, L0_tok_W2, L0_tok_b2, L0_attn_Wq, L0_attn_Wk,
           L0_attn_Wv, L0_attn_Wrk, L0_attn_r_w_bias, L0_attn_r_r_bias, L0_attn_Wo, L0_attn_bo, L0_ffn_in_weight,
           L0_ffn_in_bias, L0_ffn_out_weight):
    import concourse.bacc as bacc
    from concourse.bass_utils import run_bass_kernel_spmd

    a = np.asarray
    p = PATCHES[0]

    def chunked(w):
        return a(w).reshape(KC, DK, -1).transpose(1, 0, 2)

    def patch_weight(w, side):
        w = a(w).reshape(side, p, side, p, CH, D).transpose(1, 3, 4, 0, 2, 5)
        return w.reshape(KC, DK, side * side, D).transpose(1, 0, 2, 3)

    pix = a(x).reshape(B, 2, 4, p, 2, 4, p, CH).transpose(3, 6, 7, 2, 5, 1, 4, 0)
    pix_fine = a(x).reshape(B, GRIDS[0], p, GRIDS[0], p, CH).transpose(2, 4, 5, 0, 1, 3)
    wide = np.concatenate([a(L0_attn_Wq), a(L0_attn_Wk), a(L0_attn_Wv), a(L0_ffn_in_weight).T], axis=1)
    b_tok = np.stack([a(L0_tok_b0), a(L0_tok_b1), a(L0_tok_b2)])
    arrays = {
        "pix": pix.reshape(KC, DK, SUB, NB).transpose(1, 0, 2, 3),
        "pix_fine": pix_fine.reshape(KC, DK, B * FINE).transpose(1, 0, 2),
        "cls": np.broadcast_to(a(cls_tok)[0], (B, D)),
        "w0": chunked(L0_tok_W0),
        "w1": patch_weight(L0_tok_W1, 2),
        "w2": patch_weight(L0_tok_W2, 4),
        "b_tok": np.broadcast_to(b_tok[None], (128, 3, D)),
        "w_a": wide[0:KA],
        "w_b": np.concatenate([wide[KA:D], wide[KA:D]]),
        "w_rkt": a(L0_attn_Wrk).reshape(RF, HH, 2, KD).transpose(2, 3, 1, 0).reshape(128, HH, RF),
        "rw_bias": a(L0_attn_r_w_bias).reshape(QM, 128).T,
        "rr_bias": a(L0_attn_r_r_bias).reshape(QM, 128).T,
        "w_o": a(L0_attn_Wo).reshape(HH, 2, VD, D).transpose(1, 0, 2, 3).reshape(OC, 128, D).transpose(1, 0, 2),
        "b_o": np.broadcast_to(a(L0_attn_bo)[None], (128, D)),
        "b_in": a(L0_ffn_in_bias).reshape(MH, 128).T,
        "w_out": a(L0_ffn_out_weight).reshape(MH, 128, D).transpose(1, 0, 2),
        "ident": np.eye(128, dtype=np.float32),
        "windows": positional_windows(),
    }
    nc = bacc.Bacc("TRN2", target_bir_lowering=False, num_devices=1)
    feeds, ins = {}, {}
    for name, value in arrays.items():
        value = np.ascontiguousarray(value)
        feeds[f"in_{name}"] = value
        ins[name] = nc.dram_tensor(f"in_{name}", value.shape, mybir.dt.from_np(value.dtype), kind="ExternalInput").ap()
    out = nc.dram_tensor("out_h", (B, T, D), F32, kind="ExternalOutput").ap()
    build(nc, ins, out)
    result = run_bass_kernel_spmd(nc, [feeds], core_ids=[0])
    return result.results[0]["out_h"]
```
